# Optimizing a Trainium2 kernel written in Bass

```python
import numpy as np
import jax
import jax.numpy as jnp

def _softmax(x, axis=-1):
    return jax.nn.softmax(x, axis=axis)

def _gelu(x):
    return jax.nn.gelu(x, approximate=True)

def _silu(x):
    return jax.nn.silu(x)

def _sigmoid(x):
    return jax.nn.sigmoid(x)

def _layernorm(x, axis=-1, eps=1e-05):
    m = jnp.mean(x, axis=axis, keepdims=True)
    v = jnp.var(x, axis=axis, keepdims=True)
    return (x - m) / jnp.sqrt(v + eps)

def _scatter_add(tgt, idx, src, axis=0):
    return tgt.at[idx].add(src)

def _segment_sum(src, seg, n):
    return jax.ops.segment_sum(src, seg, n)
kernel_name = 'mk_hybrid_d1_jaxref_r8_9f4598'

def setup_inputs(seed: int=0):
    np.random.seed(seed)
    _w = jnp.asarray

    def _L0_attn_a_setup():
        import jax, jax.numpy as jnp
        import numpy as np
        import math
        N_EMBD = 128
        N_HEAD = 16
        HEAD_DIM = N_EMBD // N_HEAD
        BLOCK_SIZE = 256
        ROPE_BASE = 10000.0
        B, T = (4, 256)

        def _rope_cache(n_pos):
            theta = 1.0 / ROPE_BASE ** (jnp.arange(0, HEAD_DIM, 2, dtype=jnp.float32) / HEAD_DIM)
            idx_theta = jnp.arange(n_pos, dtype=jnp.float32)[:, None] * theta[None, :]
            return (jnp.cos(idx_theta), jnp.sin(idx_theta))

        def _apply_rope(x):
            cos, sin = _rope_cache(x.shape[1])
            cos = cos[None, :, None, :]
            sin = sin[None, :, None, :]
            xs = x.reshape(*x.shape[:-1], HEAD_DIM // 2, 2)
            x0, x1 = (xs[..., 0], xs[..., 1])
            out = jnp.stack([x0 * cos - x1 * sin, x1 * cos + x0 * sin], axis=-1)
            return out.reshape(x.shape)
        key = jax.random.key(seed)
        ks = jax.random.split(key, 5)
        x = jax.random.normal(ks[0], (B, T, N_EMBD), dtype=jnp.float32)
        s1 = 1.0 / math.sqrt(N_EMBD)
        W_attn = jax.random.uniform(ks[1], (N_EMBD, 3 * N_EMBD), jnp.float32, -s1, s1)
        b_attn = jax.random.uniform(ks[2], (3 * N_EMBD,), jnp.float32, -s1, s1)
        W_proj = jax.random.uniform(ks[3], (N_EMBD, N_EMBD), jnp.float32, -s1, s1)
        b_proj = jax.random.uniform(ks[4], (N_EMBD,), jnp.float32, -s1, s1)
        return {'x': x, 'W_attn': W_attn, 'b_attn': b_attn, 'W_proj': W_proj, 'b_proj': b_proj}
    _L0_attn_a_in = _L0_attn_a_setup()

    def _L0_attn_b_setup():
        import jax, jax.numpy as jnp
        import numpy as np
        ATT_WIDTH = 64

        def _band_mask(T, width, dtype):
            lower = width // 2
            upper = (width - 1) // 2
            i = jnp.arange(T)[:, None]
            j = jnp.arange(T)[None, :]
            keep = (i - j <= lower) & (j - i <= upper)
            return keep.astype(dtype)
        key = jax.random.key(seed)
        k1, k2, k3, k4 = jax.random.split(key, 4)
        B, T, H, D = (8, 256, 128, 128)
        scale = 1.0 / np.sqrt(H)
        return {'inputs': jax.random.normal(k1, (B, T, H), dtype=jnp.float32), 'WQ': jax.random.normal(k2, (H, D), dtype=jnp.float32) * scale, 'WK': jax.random.normal(k3, (H, D), dtype=jnp.float32) * scale, 'WV': jax.random.normal(k4, (H, D), dtype=jnp.float32) * scale}
    _L0_attn_b_in = _L0_attn_b_setup()

    def _L0_ffn_setup():
        import jax, jax.numpy as jnp
        import numpy as np
        N_HEADS = 4
        key = jax.random.key(seed)
        k1, k2, k3, k4 = jax.random.split(key, 4)
        dmodel, n_experts, expert_size = (128, 64, 128)
        B, S = (4, 256)
        x = jax.random.normal(k1, (B, S, dmodel), dtype=jnp.float32)
        expert_sel = jax.random.normal(k2, (n_experts, dmodel), dtype=jnp.float32) * dmodel ** (-0.5)
        keys = jax.random.normal(k3, (n_experts, dmodel, expert_size), dtype=jnp.float32) * dmodel ** (-0.5)
        values = jax.random.normal(k4, (n_experts, expert_size, dmodel), dtype=jnp.float32) * (n_experts * expert_size) ** (-0.5)
        return {'x': x, 'expert_sel': expert_sel, 'keys': keys, 'values': values}
    _L0_ffn_in = _L0_ffn_setup()
    _d = {'L0_attn_a_x': _L0_attn_a_in['x'], 'L0_attn_a_W_attn': _L0_attn_a_in['W_attn'], 'L0_attn_a_b_attn': _L0_attn_a_in['b_attn'], 'L0_attn_a_W_proj': _L0_attn_a_in['W_proj'], 'L0_attn_a_b_proj': _L0_attn_a_in['b_proj'], 'L0_attn_b_WQ': _L0_attn_b_in['WQ'], 'L0_attn_b_WK': _L0_attn_b_in['WK'], 'L0_attn_b_WV': _L0_attn_b_in['WV'], 'L0_ffn_expert_sel': _L0_ffn_in['expert_sel'], 'L0_ffn_keys': _L0_ffn_in['keys'], 'L0_ffn_values': _L0_ffn_in['values']}
    _x0 = _d['L0_attn_a_x']
    _d['L0_attn_a_x'] = jax.random.normal(jax.random.fold_in(jax.random.key(seed), 1), (8, 512, 128), dtype=_x0.dtype)
    del _x0
    return _d

def reference(L0_attn_a_x, L0_attn_a_W_attn, L0_attn_a_b_attn, L0_attn_a_W_proj, L0_attn_a_b_proj, L0_attn_b_WQ, L0_attn_b_WK, L0_attn_b_WV, L0_ffn_expert_sel, L0_ffn_keys, L0_ffn_values):

    def _L0_attn_a_ref(x, W_attn, b_attn, W_proj, b_proj):
        import jax, jax.numpy as jnp
        import numpy as np
        import math
        N_EMBD = 128
        N_HEAD = 16
        HEAD_DIM = N_EMBD // N_HEAD
        BLOCK_SIZE = 256
        ROPE_BASE = 10000.0
        B, T = (4, 256)

        def _rope_cache(n_pos):
            theta = 1.0 / ROPE_BASE ** (jnp.arange(0, HEAD_DIM, 2, dtype=jnp.float32) / HEAD_DIM)
            idx_theta = jnp.arange(n_pos, dtype=jnp.float32)[:, None] * theta[None, :]
            return (jnp.cos(idx_theta), jnp.sin(idx_theta))

        def _apply_rope(x):
            cos, sin = _rope_cache(x.shape[1])
            cos = cos[None, :, None, :]
            sin = sin[None, :, None, :]
            xs = x.reshape(*x.shape[:-1], HEAD_DIM // 2, 2)
            x0, x1 = (xs[..., 0], xs[..., 1])
            out = jnp.stack([x0 * cos - x1 * sin, x1 * cos + x0 * sin], axis=-1)
            return out.reshape(x.shape)
        Bx, Tx, C = x.shape
        qkv = jnp.einsum('btc,cd->btd', x, W_attn) + b_attn
        q, k, v = jnp.split(qkv, 3, axis=2)
        q = q.reshape(Bx, Tx, N_HEAD, HEAD_DIM).transpose(0, 2, 1, 3)
        k = k.reshape(Bx, Tx, N_HEAD, HEAD_DIM).transpose(0, 2, 1, 3)
        v = v.reshape(Bx, Tx, N_HEAD, HEAD_DIM).transpose(0, 2, 1, 3)
        q = _apply_rope(q)
        k = _apply_rope(k)
        scale = 1.0 / math.sqrt(HEAD_DIM)
        att = jnp.einsum('bhqd,bhkd->bhqk', q, k) * scale
        causal = jnp.tril(jnp.ones((Tx, Tx), dtype=bool))
        att = jnp.where(causal[None, None], att, -jnp.inf)
        att = jax.nn.softmax(att, axis=-1)
        y = jnp.einsum('bhqk,bhkd->bhqd', att, v)
        y = y.transpose(0, 2, 1, 3).reshape(Bx, Tx, C)
        return jnp.einsum('btc,cd->btd', y, W_proj) + b_proj

    def _L0_attn_b_ref(inputs, WQ, WK, WV):
        import jax, jax.numpy as jnp
        import numpy as np
        ATT_WIDTH = 64

        def _band_mask(T, width, dtype):
            lower = width // 2
            upper = (width - 1) // 2
            i = jnp.arange(T)[:, None]
            j = jnp.arange(T)[None, :]
            keep = (i - j <= lower) & (j - i <= upper)
            return keep.astype(dtype)
        B, T, H = inputs.shape
        D = WQ.shape[1]
        scale = jnp.asarray(D, inputs.dtype) ** 0.5
        q = jnp.einsum('bth,hd->btd', inputs, WQ)
        k = jnp.einsum('bth,hd->btd', inputs, WK)
        v = jnp.einsum('bth,hd->btd', inputs, WV)
        score = jnp.einsum('bqd,bkd->bqk', q, k) / scale
        local = _band_mask(T, ATT_WIDTH, score.dtype)
        score = score * local[None, :, :]
        attn = jax.nn.softmax(score, axis=-1)
        return jnp.einsum('bqk,bkd->bqd', attn, v)

    def _L0_ffn_ref(x, expert_sel, keys, values):
        import jax, jax.numpy as jnp
        import numpy as np
        N_HEADS = 4
        B, S, d = x.shape
        n_experts = keys.shape[0]
        xf = x.reshape(-1, d)
        N = xf.shape[0]
        logits = xf @ expert_sel.T
        sel = jax.nn.sigmoid(logits)
        sel_val, sel_idx = jax.lax.top_k(sel, N_HEADS)
        gates = jnp.zeros((N, n_experts), dtype=x.dtype)
        gates = gates.at[jnp.arange(N)[:, None], sel_idx].set(sel_val)
        h = jnp.einsum('nd,kde->nke', xf, keys)
        scores = jax.nn.relu(h) * gates[:, :, None]
        out = jnp.einsum('nke,kev->nv', scores, values)
        return out.reshape(B, S, -1)
    x = L0_attn_a_x
    x = x + _L0_attn_a_ref(_layernorm(x, axis=-1), L0_attn_a_W_attn, L0_attn_a_b_attn, L0_attn_a_W_proj, L0_attn_a_b_proj)
    x = x + _L0_ffn_ref(_layernorm(x, axis=-1), L0_ffn_expert_sel, L0_ffn_keys, L0_ffn_values)
    x = x + _L0_attn_b_ref(_layernorm(x, axis=-1), L0_attn_b_WQ, L0_attn_b_WK, L0_attn_b_WV)
    x = x + _L0_ffn_ref(_layernorm(x, axis=-1), L0_ffn_expert_sel, L0_ffn_keys, L0_ffn_values)
    return x

_drawn_inputs = setup_inputs


def setup_inputs(seed=0):
    import zlib

    import numpy as np

    out = dict(_drawn_inputs(seed))
    spreads = {}
    factors = {}
    for name, (base, spread) in spreads.items():
        noise = np.random.default_rng([zlib.crc32(name.encode()), seed]).standard_normal(out[name].shape)
        drawn = base * np.exp(spread * noise) if base else spread * noise
        out[name] = jnp.asarray(drawn.astype(out[name].dtype))
    for name, factor in factors.items():
        out[name] = (out[name] * factor).astype(out[name].dtype)
    return out
```

```python
from contextlib import ExitStack

import concourse.bass as bass
from concourse import mybir

F32 = mybir.dt.float32
BF16 = mybir.dt.bfloat16
I32 = mybir.dt.int32
U32 = mybir.dt.uint32
ALU = mybir.AluOpType
ACT = mybir.ActivationFunctionType
AX = mybir.AxisListType
ENG = mybir.EngineType

P = 128
B, T, C = 8, 512, 128
TT = T // P
NT = B * TT
NH, HD = 16, 8
NP = NH // 2
NE, TOPK = 64, 4
ROWS = B * T * TOPK
REGION = B * T + P
ROW = C + 4
NTILES = (ROWS - NE) // P + NE + 1
NTILES += -NTILES % 32
DUMMY = NE * REGION // P
NOWHERE = 1 << 20
EPS = 1e-5
SCALE_A = float(HD) ** -0.5
SCALE_B = float(C) ** -0.5
NEG = -1e30

JOBS = [
    (0, "MROW1", 0), (0, "XT", 2),
    (1, "NT", -2), (1, "Q", 2), (1, "K", 2),
    (2, "LG", -2),
    (3, "V", 1), (3, "Y0", -1),
    (4, "MROW0", 1), (4, "RK", -2), (4, "Y1", -1),
    (5, "Y2", -1), (5, "Y3", -1),
    (6, "YT", -1),
    (7, "PJ", -1),
]
FIRST_IT, LAST_IT = -3, B + 2


def job_numbers():
    n, out = 0, {}
    for it in range(FIRST_IT, LAST_IT + 1):
        for _, name, off in JOBS:
            if 0 <= it + off < B:
                out[name, it + off] = n
                n += 1
    return out


BJOBS = [(0, "XT", 0), (0, "NT", -1), (1, "Q", 0), (2, "K", 0), (3, "V", 0), (1, "LG", -1),
         (4, "S0", 0), (5, "S1", 0), (6, "P0", 0), (7, "O0", 0), (4, "S2", 0), (6, "P1", 0), (7, "O1", 0),
         (2, "RK", -1), (5, "S3", 0), (6, "P2", 0), (7, "O2", 0), (6, "P3", 0), (7, "O3", 0)]
LAST_IT_B = B + 1
G = 4
U = 8
ROUNDS = NTILES // (G * U)
GROUPS = NTILES // G


def bank_numbers():
    n, out = [0] * 8, {}
    for it in range(LAST_IT_B + 1):
        for bank, name, off in BJOBS:
            if 0 <= it + off < B:
                out[name, it + off] = bank, n[bank]
                n[bank] += 1
    return out


def slots():
    for it in range(FIRST_IT, LAST_IT + 1):
        for k in range(8):
            yield it, k


def build(nc, x_d, w_d, bcol_d, bv_d, wproj_d, bproj_d, trig_row_d, trig_col_d, wqkv_b_d, esel_d, keys_d, values_d, out_d):
    job = job_numbers()
    bjob = bank_numbers()
    with ExitStack() as ctx:
        def sb(name, shape, dt=F32):
            return ctx.enter_context(nc.sbuf_tensor(name, shape, dt))

        def sem(name):
            return ctx.enter_context(nc.semaphore(name))

        qd = nc.dram_tensor("q_parts", [2, NH, 64, T], BF16).ap()
        kd = nc.dram_tensor("k_parts", [2, NH, 64, T], BF16).ap()
        md = nc.dram_tensor("max_rows", [4, 32, T], BF16).ap()
        sorted_d = [nc.dram_tensor(f"sorted_rows{l}", [NE * REGION + P, ROW], F32).ap() for l in range(2)]
        result_d = [nc.dram_tensor(f"result_rows{l}", [ROWS, C], F32).ap() for l in range(2)]

        x = sb("x_res", [P, NT, C])
        arena = sb("arena", [P, 22528])
        prob = arena[:, 0:10240].rearrange("p (g r n) -> p g r n", g=2, r=2)
        kw = arena[:, 0:8192]
        vw = arena[:, 8192:16384]
        pads = arena[0:32, 16384:16384 + 4 * ROW]
        band = arena[:, 20608:21632].bitcast(BF16).rearrange("p (t n) -> p t n", t=TT)
        qs = arena[:, 10240:14336].bitcast(BF16).rearrange("p (s r n) -> p s r n", s=4, r=4)
        kz = arena[:, 14336:22528].bitcast(BF16).rearrange("p (s h r n) -> p s h r n", s=4, h=2, r=4)
        vaug = sb("v_aug", [P, 2, TT, NH, 32])
        yts = sb("y_heads", [P, 2, 4, T])
        xs = sb("x_send", [P, 2, TT, TOPK, ROW])
        w = sb("w_attn", [P, 5 * C])
        wrot = sb("w_rotated", [P, 2, C])
        wqk = sb("w_qk", [P, 2, C])
        bcol = sb("b_cols", [P, 4])
        brot = sb("b_rotated", [P, 3])
        bqk = sb("b_qk", [P, 2])
        bv = sb("b_v", [P, C])
        wproj = sb("w_proj", [P, C])
        bproj = sb("b_proj", [P, C])
        trig_row = sb("trig_row", [P, 2, C])
        trig_col = sb("trig_col", [P, 2])
        wb = sb("w_b", [P, 3 * C])
        esel = sb("expert_sel", [P, NE])
        ident = sb("ident", [P, P])
        identb = sb("identb", [P, P], BF16)
        maskneg = sb("maskneg", [P, P], BF16)
        tri = sb("tri", [P, P], BF16)
        onesb = sb("onesb", [P, P], BF16)
        iota_e = sb("iota_e", [P, NE])
        ebase = sb("ebase", [P, NE])
        xn0 = sb("xn0", [P, TT, C])
        xn1 = sb("xn1", [P, TT, C])
        st0 = sb("st0", [P, TT, 6])
        mv0 = sb("mv0", [P, TT, 2])
        rs0 = sb("rs0", [P, TT])
        st1 = sb("st1", [P, TT, 6])
        mv1 = sb("mv1", [P, TT, 2])
        rs1 = sb("rs1", [P, TT])
        mhalf = sb("minus_half", [P, TT])
        xnt = sb("xnt", [P, 2, T])
        ropea = sb("rope_a", [P, 2, T])
        ropeb = sb("rope_b", [P, 2, T])
        parth = sb("part_h", [P, 2, T], BF16)
        partm = sb("part_m", [P, 2, T], BF16)
        partl = sb("part_l", [P, 2, T], BF16)
        czero, cone = parth[:, 0, :], partm[0:48, 0, :]
        mx = sb("row_max", [P, TT, 8])
        mneg = sb("row_neg", [P, TT, 8])
        mres = sb("row_rest", [P, TT, 8])
        mparts = sb("max_parts", [P, TT, 8, 4], BF16)
        mt = sb("max_t", [32, 2, T], BF16)
        yrc = sb("y_recip", [P, NH])
        ytok = sb("y_tok", [P, TT, C])
        yt2 = sb("y_t", [P, T])
        ntt = sb("xn1_t", [P, T])
        sg = sb("sigmoid", [P, TT, NE])
        top = sb("gates", [P, NT, 8])
        idx8 = sb("idx8", [P, TT, 8], U32)
        idxf = sb("idxf", [P, TT, TOPK])
        oh = sb("one_hot", [P, TT, TOPK, NE], BF16)
        msum = sb("chosen", [P, TT, NE], BF16)
        acc = sb("chosen_before", [P, 2, NE], BF16)
        tsum = sb("chosen_now", [P, NE], BF16)
        rpos = sb("rank_pos", [P, TT, NE])
        prod = sb("pos_prod", [P, TT, TOPK, NE])
        destf = sb("dest_f", [P, TT * TOPK])
        dest = sb("dest", [P, NT * TOPK], I32)
        trii = sb("tri_incl", [P, P], BF16)
        iota_t = sb("iota_tiles", [NE, NTILES])
        count = sb("count", [NE, 1])
        padrow = sb("pad_row", [1, NE], I32)
        ceil_i = sb("ceil_i", [NE, 1], I32)
        ceil_s = sb("ceil_s", [NE, 1], I32)
        ntile = sb("tiles_of", [NE, 1], BF16)
        skip = sb("skip_of", [NE, 1], BF16)
        upto = sb("tiles_upto", [NE, 1])
        rowf = w[0:1, 0:NTILES]
        tile_e = w[0:1, NTILES:2 * NTILES].bitcast(I32)
        tile_r = w[0:1, 2 * NTILES:3 * NTILES].bitcast(I32)
        past = trig_row[0:NE, 0, 0:NTILES // 2].bitcast(BF16)
        xsf = xs[:, :, :, :, :].rearrange("p b t s n -> p (b t s n)")
        xin = xsf[:, 0:U * G * ROW].rearrange("p (u n) -> p u n", u=U * G)
        yout = vaug[:, :, :, :, :].rearrange("p b t h d -> p (b t h d)")[:, 0:U * G * C].rearrange("p (u n) -> p u n", u=U * G)
        ytf = yts[:, :, :, :].rearrange("p b g n -> p (b g) n")
        xtt, ktile, hidt = ytf[:, 0:2, :], ytf[:, 2:4, :], ytf[:, 4:6, :]
        yg = vaug[:, :, :, :, :].rearrange("p b t h d -> p b t (h d)")
        masked = ytf[:, 0:2, :]
        probb = ytf[:, 2:4, :]
        probt = ytf[:, 4:6, :]
        rowmax = sb("row_max_b", [P, TT])
        nrow = sb("neg_max_b", [P, TT])
        rowsum = sb("row_sum_b", [P, TT])
        rinv = sb("row_inv_b", [P, TT])

        ps = ctx.enter_context(nc.psum_tensor("ps", [P, 8, 512], F32))
        misc = ps[:, 7, :]
        miscb = ps[0:32, 7, :].bitcast(BF16)
        pv = ps[:, 6, :]

        in_x = sem("in_x")
        in_w = sem("in_w")
        consts = sem("consts")
        consts_v = sem("consts_v")
        rows_init = sem("rows_init")
        misc_ready = sem("misc_ready")
        misc_free = sem("misc_free")
        ln0 = sem("ln0")
        ln1 = sem("ln1")
        rotated = sem("rotated")
        rstd0 = sem("rstd0")
        rstd1 = sem("rstd1")
        xb_done = sem("xb_done")
        pool_split = sem("pool_split")
        act_split = sem("act_split")
        parts_out = sem("parts_out")
        qk_landed = [sem(f"qk_landed{i}") for i in range(4)]
        s1_ready = sem("s1_ready")
        s1_free = sem("s1_free")
        mrow_seq = sem("mrow_seq")
        mrow_out = [sem(f"mrow_out{i}") for i in range(2)]
        mrow_landed = [sem(f"mrow_landed{i}") for i in range(4)]
        s2_ready = sem("s2_ready")
        exp_done = sem("exp_done")
        sel_done = sem("sel_done")
        pv_done = sem("pv_done")
        pv_evac = sem("pv_evac")
        yrc_done = sem("yrc_done")
        xs_filled = sem("xs_filled")
        meta_done = sem("meta_done")
        top_seq = sem("top_seq")
        oh_done = sem("oh_done")
        msum_done = sem("msum_done")
        acc_seq = sem("acc_seq")
        prod_done = sem("prod_done")
        dest_seq = sem("dest_seq")
        sent = [sem(f"sent{i}") for i in range(2)]
        done_out = sem("done_out")
        bank_ready = [sem(f"bank_ready{i}") for i in range(8)]
        bank_free = [sem(f"bank_free{i}") for i in range(8)]
        tab_pe = sem("tab_pe")
        tab_v = sem("tab_v")
        pads_made = sem("pads_made")
        padded = sem("padded")
        band_made = sem("band_made")
        dummy_out = sem("dummy_out")
        ew_in = sem("expert_weights_in")
        x_in = [sem(f"x_in{i}") for i in range(U)]
        t1_ready, t1_done = sem("t1_ready"), sem("t1_done")
        h_ready, h_done = sem("h_ready"), sem("h_done")
        ktile_done = sem("ktile_done")
        y_ready, y_done = sem("y_ready"), sem("y_done")
        y_sent = [sem(f"y_sent{i}") for i in range(U)]
        yg_in = [sem(f"yg_in{i}") for i in range(2)]
        combined = sem("combined")
        ln2 = sem("ln2")
        ln3 = sem("ln3")
        rstd2 = sem("rstd2")
        rstd3 = sem("rstd3")
        mask_done = sem("mask_done")
        nrow_done = sem("nrow_done")
        expb_done = sem("expb_done")
        rinv_done = sem("rinv_done")
        NTAB = 11
        NCONST = 11
        NCONSTV = 9

        def scatter_chunk(it, k):
            return (it - 2, 0) if k == 7 else (it - 3, k + 1)

        def expert_rounds(eng, step, tail, peeled=1):
            for s in range(U * peeled):
                step(s, s % U, s // U)
            with eng.Fori(peeled, ROUNDS) as rnd:
                for u in range(U):
                    step(rnd * U + u, u, rnd)
            for s in range(tail):
                step(GROUPS + s, s, ROUNDS)

        def column_of(engine, tile):
            return nc.values_load(tile_e[0:1, bass.ds(tile, 1)], (engine,), min_val=0, max_val=C * (NE - 1),
                                  skip_runtime_bounds_check_because="the tile table is clipped to the last expert")

        def row_of(engine, table, n, most):
            return nc.values_load(table[0:1, bass.ds(n, 1)], (engine,), min_val=0, max_val=most,
                                  skip_runtime_bounds_check_because="the tables are within the sorted rows")

        def pad(eng, engine, layer, first):
            eng.wait_ge(pads_made, 2)
            eng.wait_ge(tab_v, NTAB * layer + 2)
            with eng.Fori(first, first + NE // 2) as e:
                row = row_of(engine, padrow, e, NE * REGION)
                eng.dma_start(sorted_d[layer][bass.ds(row, P), :].rearrange("(a b) n -> a (b n)", b=4), pads).then_inc(padded, 16)

        block = ctx.enter_context(nc.Block())

        @block.sync
        def _(sp):
            sp.dma_start(x[:, 0:TT, :], x_d.rearrange("(t p) c -> p t c", p=P)[:, 0:TT, :]).then_inc(in_x, 16)
            for dst, src in ((w[:, :], w_d), (bcol[:, :], bcol_d), (trig_col[:, :], trig_col_d),
                             (trig_row[:, :, :].rearrange("p a c -> p (a c)"), trig_row_d.unsqueeze(0).broadcast_to([P, 2 * C]))):
                sp.dma_start(dst, src).then_inc(in_w, 16)
            sp.dma_start(x[:, TT:, :], x_d.rearrange("(t p) c -> p t c", p=P)[:, TT:, :]).then_inc(in_x, 16)
            sp.dma_start(bv[:, :], bv_d.unsqueeze(0).broadcast_to([P, C])).then_inc(in_w, 16)
            sp.dma_start(bproj[:, :], bproj_d.unsqueeze(0).broadcast_to([P, C])).then_inc(in_w, 16)
            for dst, src in ((wproj[:, :], wproj_d), (wb[:, :], wqkv_b_d), (esel[:, :], esel_d)):
                sp.dma_start(dst, src).then_inc(in_w, 16)
            sp.wait_ge(consts_v, NCONSTV)
            for par in range(2):
                for d in (qd, kd):
                    sp.dma_start(d[par, :, 56:64, :], czero).then_inc(rows_init, 16)
                sp.dma_start(qd[par, :, 32:40, :], czero).then_inc(rows_init, 16)
                sp.dma_start(kd[par, :, 35:40, :], czero[0:80, :]).then_inc(rows_init, 16)
                sp.dma_start(kd[par, :, 32:35, :], cone).then_inc(rows_init, 16)

            def write_parts(b):
                par = b % 2
                sp.wait_ge(act_split, 4 * b + 4)
                sp.wait_ge(pool_split, 4 * b + 4)
                if b >= 2:
                    for g in (2 * b - 4, 2 * b - 3):
                        sp.wait_ge(qk_landed[g % 4], 48 * (g // 4 + 1))
                for d, n, groups in ((qd, 0, (parth, parth, parth, partm, None, partm, partl)),
                                     (kd, 1, (partl, partm, parth, parth, None, partm, parth))):
                    for gi, part in enumerate(groups):
                        if part is not None:
                            sp.dma_start(d[par, :, 8 * gi:8 * gi + 8, :], part[:, n, :]).then_inc(parts_out, 16)

            def load_parts(g):
                b, hf, s = g // 2, g % 2, g % 4
                sp.wait_ge(parts_out, 192 * (b + 1))
                sp.wait_ge(rows_init, 160)
                if g >= 4:
                    sp.wait_ge(s2_ready, 12 * (g - 3))
                hs = slice(8 * hf, 8 * hf + 8)
                sp.dma_start(qs[:, s, :, :], qd[b % 2, hs].rearrange("(r h) q n -> (h q) r n", h=2)).then_inc(qk_landed[s], 16)
                for hb in range(2):
                    sp.dma_start(kz[64 * hb:64 * hb + 64, s, hb, :, :],
                                 kd[b % 2, hs].rearrange("(r h) q n -> h q r n", h=2)[hb]).then_inc(qk_landed[s], 16)

            def max_rows(g):
                name = ("MROW1" if g % 2 else "MROW0", g // 2)
                s = g % 4
                sp.wait_ge(misc_free, job[name] + 1)
                sp.dma_start(md[s], mt[:, g % 2, :]).then_inc(mrow_out[g % 2], 16)
                sp.wait_ge(mrow_out[g % 2], 16 * (g // 2 + 1))
                for hb in range(2):
                    sp.dma_start(qs[64 * hb + 32:64 * hb + 36, s, :, :],
                                 md[s].rearrange("(r h q) n -> h q r n", h=2, q=4)[hb]).then_inc(mrow_landed[s], 16)

            for it, k in slots():
                if k == 0 and 0 <= it < B:
                    max_rows(2 * it + 1)
                if k == 3 and 0 <= it + 2 < B:
                    write_parts(it + 2)
                if k == 4:
                    if 0 <= it + 1 < B:
                        max_rows(2 * it + 2)
                    if 0 <= it + 2 < B:
                        load_parts(2 * it + 4)
                if k == 7 and 0 <= it + 2 < B:
                    load_parts(2 * it + 5)

            sp.wait_ge(s2_ready, 3 * B * NP)
            sp.wait_ge(s1_ready, 5 * B * NP)
            sp.wait_ge(pv_done, 4 * B)
            for e in range(0, NE, 16):
                for dst, src in ((kw, keys_d), (vw, values_d)):
                    sp.dma_start(dst[:, C * e:C * (e + 16)].rearrange("p (e n) -> p e n", e=16),
                                 src[e:e + 16].rearrange("e p n -> p e n")).then_inc(ew_in, 16)

            def expert_loads(layer):
                pad(sp, ENG.SP, layer, 0)
                for i in range(2):
                    sp.wait_ge(sent[i], 256 * (B // 2) * (layer + 1))
                sp.wait_ge(padded, 16 * NE * (layer + 1))
                sp.wait_ge(dummy_out, 32)
                sp.wait_ge(tab_v, NTAB * (layer + 1))

                def load(s, u, rnd):
                    if layer or not isinstance(s, int):
                        sp.wait_ge(y_sent[u], (rnd + ROUNDS * layer) * (16 * G))
                    for i in range(G):
                        row = row_of(ENG.SP, tile_r, s * G + i, NE * REGION)
                        sp.dma_start(xin[:, G * u + i, :], sorted_d[layer][bass.ds(row, P), :]).then_inc(x_in[u], 16)

                expert_rounds(sp, load, 0)

            def results(layer, b):
                if b == 0:
                    for u in range(U):
                        sp.wait_ge(y_sent[u], 16 * G * ROUNDS * (layer + 1))
                n = B * layer + b
                if n >= 2:
                    sp.wait_ge(combined, 16 * (n - 1))
                sp.dma_start(yg[:, b % 2, :, :], result_d[layer].rearrange("(n p s) c -> p n (s c)", p=P, s=TOPK)[:, TT * b:TT * b + TT, :]
                             ).then_inc(yg_in[b % 2], 16)

            sp.wait_ge(pads_made, 2)
            for layer in range(2):
                sp.dma_start(sorted_d[layer][NE * REGION:NE * REGION + P, :].rearrange("(a b) n -> a (b n)", b=4), pads).then_inc(dummy_out, 16)
            expert_loads(0)
            for b in range(B):
                results(0, b)
            expert_loads(1)
            for b in range(B):
                results(1, b)
                if b:
                    sp.wait_ge(combined, 16 * (B + b))
                    sp.dma_start(out_d.rearrange("(t p) c -> p t c", p=P)[:, TT * (b - 1):TT * b, :],
                                 x[:, TT * (b - 1):TT * b, :]).then_inc(done_out, 16)
            sp.wait_ge(combined, 16 * 2 * B)
            sp.dma_start(out_d.rearrange("(t p) c -> p t c", p=P)[:, TT * (B - 1):, :], x[:, TT * (B - 1):, :]).then_inc(done_out, 16)
            sp.wait_ge(done_out, 16 * B)

        @block.tensor
        def _(pe):
            def begin(name, b):
                n = job[name, b]
                if n:
                    pe.wait_ge(misc_free, n)

            def scores_kq(pr):
                g, p = pr // 4, pr % 4
                s = g % 4
                if p == 0:
                    pe.wait_ge(mrow_landed[s], 32 * (g // 4 + 1))
                for u in range(3):
                    v = 3 * pr + u
                    if v >= 2:
                        pe.wait_ge(exp_done, v - 1)
                    base = 2 * (v % 2)
                    parts = [(u, 0, base, 0), (u, 1, base + 1, 0), (u, 3, base + 1, 384)] if u < 2 else \
                        [(0, 2, base, 0), (1, 2, base, 256)]
                    for hb, j, bank, at in parts:
                        n = T - P * j
                        mm = pe.matmul(ps[:, bank, at:at + n], kz[:, s, hb, p, P * j:P * j + P],
                                       qs[:, s, p, P * j:T], start=True, stop=True)
                    mm.then_inc(s2_ready, 1)

            def scores_qk(pr):
                g, p = pr // 4, pr % 4
                s = g % 4
                if p == 0:
                    pe.wait_ge(qk_landed[s], 48 * (g // 4 + 1))
                for u, parts in enumerate([[(0, 3, 0)], [(0, 0, 0), (0, 2, 128)], [(1, 3, 0)],
                                           [(1, 0, 0), (1, 2, 128)], [(0, 1, 0), (1, 1, 256)]]):
                    n = 5 * pr + u
                    if n >= 2:
                        pe.wait_ge(s1_free, n - 1)
                    for hb, i, at in parts:
                        m = P * (i + 1)
                        pe.matmul(ps[:, 4 + n % 2, at:at + m], qs[:, s, p, P * i:P * i + P], kz[:, s, hb, p, 0:m],
                                  start=True, stop=False)
                        mm = pe.matmul(ps[:, 4 + n % 2, at + m - P:at + m], identb[:, :], maskneg[:, :],
                                       start=False, stop=True)
                    mm.then_inc(s1_ready, 1)

            def values(grp):
                b = grp // 4
                pe.wait_ge(sel_done, 2 * grp + 2)
                pe.wait_ge(misc_free, job["V", b] + 1)
                if grp:
                    pe.wait_ge(pv_evac, grp)
                for j, width in ((0, 512), (1, 384), (2, 256), (3, 128)):
                    for q in range(4):
                        hb = q % 2
                        at = {0: 1024 * hb, 1: 1024 * hb + 512, 3: 1024 * hb + 896, 2: 2048 + 256 * hb}[j]
                        mm = pe.matmul(ps[32 * q:32 * q + 32, 6, P * j:T],
                                       vaug[:, b % 2, j, 4 * (grp % 4) + q, :],
                                       prob[:, grp % 2, q // 2, at:at + width], start=(j == 0), stop=(j == 3))
                mm.then_inc(pv_done, 1)

            def logits(bank):
                for t in range(TT):
                    mm = pe.matmul(bank[:, NE * t:NE * t + NE], ntt[:, P * t:P * t + P], esel[:, :], start=True, stop=True)
                return mm

            def ranks(bank, layer, b):
                n = B * layer + b
                pe.wait_ge(msum_done, n + 1)
                if n:
                    pe.wait_ge(acc_seq, 2 * n)
                for t in range(TT):
                    o = bank[:, NE * t:NE * t + NE]
                    pe.matmul(o, tri[:, :], msum[:, t, :], start=True, stop=False)
                    for e in range(t):
                        pe.matmul(o, onesb[:, :], msum[:, e, :], start=False, stop=False)
                    mm = pe.matmul(o, onesb[:, :], acc[:, layer, :], start=False, stop=True)
                return mm

            def run(name, b):
                begin(name, b)
                if name[:4] == "MROW":
                    g = 2 * b + (name == "MROW1")
                    pe.wait_ge(mrow_seq, 5 * g + 5)
                    for i in range(TT):
                        mm = pe.transpose(miscb[:, P * i:P * i + P], mparts[:, i, :, :].rearrange("p h s -> p (h s)"), identb[:, :])
                elif name in ("XT", "NT", "YT"):
                    src = {"XT": xn0, "NT": xn1, "YT": ytok}[name]
                    if name != "YT":
                        pe.wait_ge(ln0 if name == "XT" else ln1, 13 * b + 13)
                    for t in range(TT):
                        mm = pe.transpose(misc[:, P * t:P * t + P], src[:, t, :], ident[:, :])
                elif name in ("Q", "K"):
                    pe.wait_ge(rotated, 12)
                    mm = pe.matmul(misc, wqk[:, "QK".index(name), :], xnt[:, b % 2, :], start=True, stop=True)
                elif name == "V":
                    for t in range(TT):
                        mm = pe.matmul(misc[:, P * t:P * t + P], xnt[:, b % 2, P * t:P * t + P], w[:, 4 * C:], start=True, stop=True)
                elif name[0] == "Y":
                    i = int(name[1])
                    for n in range(4):
                        mm = pe.transpose(misc[:, P * n:P * n + P], yts[:, b % 2, n, P * i:P * i + P], ident[:, :])
                elif name == "PJ":
                    for t in range(TT):
                        mm = pe.matmul(misc[:, P * t:P * t + P], yt2[:, P * t:P * t + P], wproj[:, :], start=True, stop=True)
                elif name == "LG":
                    mm = logits(misc)
                elif name == "RK":
                    mm = ranks(misc, 0, b)
                mm.then_inc(misc_ready, 1)

            pe.wait_ge(in_w, 16 * 9)
            pe.wait_ge(consts, NCONST)
            pe.wait_ge(consts_v, NCONSTV)
            for it, k in slots():
                pr = 8 * it + k
                if 0 <= pr < B * NP:
                    scores_kq(pr)
                if 0 <= pr + NP < B * NP:
                    scores_qk(pr + NP)
                if k % 2 and 0 <= pr - 3 < B * NP:
                    values((pr - 3) // 2)
                for slot, name, off in JOBS:
                    if slot == k and 0 <= it + off < B:
                        if name == "Y0":
                            pe.wait_ge(pv_evac, 4 * (it + off) + 4)
                        run(name, it + off)

            def tile_table(layer):
                bank = ps[:, 6, :]
                pe.wait_ge(acc_seq, 2 * B * (layer + 1))
                if layer:
                    pe.wait_ge(bank_free[6], bjob["P3", B - 1][1] + 1)
                else:
                    pe.wait_ge(pv_evac, 4 * B)
                v = NTAB * layer
                pe.matmul(bank[0:1, 384:384 + NE], onesb[:, 0:1], acc[:, layer, :], start=True, stop=True)
                pe.matmul(bank[0:NE, 0:1], acc[:, layer, :], onesb[:, 0:1], start=True, stop=True).then_inc(tab_pe, 1)
                pe.wait_ge(tab_v, v + 6)
                pe.matmul(bank[0:NE, 0:1], trii[0:NE, 0:NE], ntile[:, :], start=True, stop=True).then_inc(tab_pe, 1)
                pe.wait_ge(tab_v, v + 8)
                pe.matmul(bank[0:1, 0:NTILES], onesb[0:NE, 0:1], past, start=True, stop=True)
                pe.matmul(bank[0:1, NTILES:2 * NTILES], skip[:, :], past, start=True, stop=True).then_inc(tab_pe, 1)

            def experts(layer):
                pe.wait_ge(tab_v, NTAB * (layer + 1))
                base = GROUPS * layer
                if layer:
                    for i in range(6):
                        pe.wait_ge(bank_free[i], max(n for k, n in bjob.values() if k == i) + 1)
                else:
                    pe.wait_ge(exp_done, 3 * B * NP)
                    pe.wait_ge(s1_free, 5 * B * NP)
                    pe.wait_ge(ew_in, 16 * 8)

                def step(s, u, rnd):
                    static = isinstance(s, int)

                    def late(n):
                        return layer or not static or s >= n

                    def here(n):
                        return not static or 0 <= s - n < GROUPS

                    if here(0):
                        pe.wait_ge(x_in[u], (rnd + ROUNDS * layer + 1) * (16 * G))
                        if late(2):
                            pe.wait_ge(t1_done, s + (base - 1))
                        for i in range(G):
                            mm = pe.transpose(ps[:, u % 2, P * i:P * i + P], xin[:, G * u + i, 0:C], ident[:, :])
                        mm.then_inc(t1_ready, 1)
                    if here(1):
                        v = (u + 1) % 2
                        pe.wait_ge(t1_done, s + base)
                        pe.wait_ge(ktile_done, s + base)
                        if late(3):
                            pe.wait_ge(h_done, s + (base - 2))
                        for i in range(G):
                            mm = pe.matmul(ps[:, 2 + v, P * i:P * i + P], ktile[:, v, P * i:P * i + P], xtt[:, v, P * i:P * i + P],
                                           start=True, stop=True)
                        mm.then_inc(h_ready, 1)
                    if here(2):
                        v = u % 2
                        pe.wait_ge(h_done, s + (base - 1))
                        if late(4):
                            pe.wait_ge(y_done, s + (base - 3))
                        for i in range(G):
                            col = column_of(ENG.PE, (s - 2) * G + i)
                            mm = pe.matmul(ps[:, 4 + v, P * i:P * i + P], hidt[:, v, P * i:P * i + P], vw[:, bass.ds(col, C)],
                                           start=True, stop=True)
                        mm.then_inc(y_ready, 1)

                expert_rounds(pe, step, 2)

            def attention_b(name, b):
                bank, n = bjob[name, b]
                o = ps[:, bank, :]
                if n:
                    pe.wait_ge(bank_free[bank], n)
                elif bank < 6:
                    pe.wait_ge((t1_done, h_done, y_done)[bank // 2], GROUPS)
                elif bank == 6:
                    pe.wait_ge(tab_v, NTAB)
                else:
                    pe.wait_ge(misc_free, len(job))
                i = int(name[1]) if name[0] in "SPO" else 0
                if name == "XT":
                    pe.wait_ge(ln2, 13 * b + 13)
                    for t in range(TT):
                        mm = pe.transpose(o[:, P * t:P * t + P], xn0[:, t, :], ident[:, :])
                elif name == "NT":
                    pe.wait_ge(ln3, 13 * b + 13)
                    for t in range(TT):
                        mm = pe.transpose(o[:, P * t:P * t + P], xn1[:, t, :], ident[:, :])
                elif name in ("Q", "K"):
                    pe.wait_ge(bank_free[0], bjob["XT", b][1] + 1)
                    c = C * "QK".index(name)
                    mm = pe.matmul(o, wb[:, c:c + C], xnt[:, 0, :], start=True, stop=True)
                elif name == "V":
                    for t in range(TT):
                        mm = pe.matmul(o[:, P * t:P * t + P], xnt[:, 0, P * t:P * t + P], wb[:, 2 * C:], start=True, stop=True)
                elif name == "LG":
                    pe.wait_ge(bank_free[0], bjob["NT", b][1] + 1)
                    mm = logits(o)
                elif name == "RK":
                    mm = ranks(o, 1, b)
                elif name[0] == "S":
                    pe.wait_ge(bank_free[1], bjob["Q", b][1] + 1)
                    pe.wait_ge(bank_free[2], bjob["K", b][1] + 1)
                    mm = pe.matmul(o, ropea[:, 0, P * i:P * i + P], ropea[:, 1, :], start=True, stop=True)
                elif name[0] == "P":
                    pe.wait_ge(expb_done, TT * b + i + 1)
                    for j in range(TT):
                        mm = pe.transpose(o[:, P * j:P * j + P], probb[:, i % 2, P * j:P * j + P], ident[:, :])
                elif name[0] == "O":
                    pe.wait_ge(bank_free[6], bjob[f"P{i}", b][1] + 1)
                    pe.wait_ge(bank_free[3], bjob["V", b][1] + 1)
                    for j in range(TT):
                        mm = pe.matmul(o[:, 0:C], probt[:, i % 2, P * j:P * j + P], ropeb[:, 0, P * j:P * j + P],
                                       start=(j == 0), stop=(j == TT - 1))
                mm.then_inc(bank_ready[bank], 1)

            tile_table(0)
            experts(0)
            for it in range(LAST_IT_B + 1):
                for _, name, off in BJOBS:
                    if 0 <= it + off < B:
                        attention_b(name, it + off)
            tile_table(1)
            experts(1)

        @block.scalar
        def _(act):
            def take(name, b):
                act.wait_ge(misc_ready, job[name, b] + 1)

            for it, k in slots():
                pr = 8 * it + k
                if 0 <= pr < B * NP:
                    grp = pr // 2
                    if pr % 2 == 0 and grp >= 2:
                        act.wait_ge(pv_done, grp - 1)
                    for u in range(3):
                        v = 3 * pr + u
                        act.wait_ge(s2_ready, v + 1)
                        base = 2 * (v % 2)
                        src = ps[:, base:base + 2, :] if u < 2 else ps[:, base, :]
                        n = 1024 if u < 2 else 512
                        dst = prob[:, grp % 2, pr % 2, 1024 * u:1024 * u + n]
                        if u < 2:
                            dst = dst.rearrange("p (a n) -> p a n", a=2)
                        nc.scalar.activation(dst, src, ACT.Exp, scale=SCALE_A).then_inc(exp_done, 1)
                if k % 2 and 0 <= pr - 3 < B * NP:
                    grp = (pr - 3) // 2
                    b = grp // 4
                    act.wait_ge(pv_done, grp + 1)
                    if b >= 2:
                        act.wait_ge(misc_ready, job["Y3", b - 2] + 1)
                    nc.scalar.copy(yts[:, b % 2, grp % 4, :], pv).then_inc(pv_evac, 1)
                if k == 0:
                    if 0 <= it < B:
                        g = 2 * it + 1
                        take("MROW1", it)
                        if g >= 2:
                            act.wait_ge(mrow_out[1], 16 * (g // 2))
                        nc.scalar.copy(mt[:, 1, :], miscb[:, 0:T]).then_inc(misc_free, 1)
                    if 0 <= it + 2 < B:
                        b = it + 2
                        take("XT", b)
                        nc.scalar.copy(xnt[:, b % 2, :], misc).then_inc(misc_free, 1)
                if k == 1:
                    if 0 <= it - 2 < B:
                        b = it - 2
                        take("NT", b)
                        nc.scalar.copy(ntt[:, :], misc).then_inc(misc_free, 1)
                        if b >= 2:
                            act.wait_ge(sent[b % 2], 256 * (b // 2))
                        for t in range(TT):
                            nc.scalar.copy(xs[:, b % 2, t, :, 0:C],
                                           xn1[:, t, :].unsqueeze(1).broadcast_to([P, TOPK, C])).then_inc(xs_filled, 1)
                if k == 2 and 0 <= it - 2 < B:
                    b = it - 2
                    take("LG", b)
                    if b:
                        act.wait_ge(top_seq, 11 * (b - 1) + 10)
                    nc.scalar.activation(sg[:, :, :].rearrange("p t e -> p (t e)"), misc[:, 0:TT * NE], ACT.Exp,
                                         scale=-1.0).then_inc(misc_free, 1)
                if k == 2 and 0 <= it + 2 < B:
                    b = it + 2
                    act.wait_ge(misc_free, job["K", b] + 1)
                    act.wait_ge(rows_init, 160)
                    if b:
                        act.wait_ge(parts_out, 192 * b)
                    for n in range(2):
                        nc.scalar.copy(parth[:, n, :], ropea[:, n, :]).then_inc(act_split, 1)
                if k == 3 and 0 <= it + 2 < B:
                    b = it + 2
                    for n in range(2):
                        act.wait_ge(pool_split, 4 * b + 1 + n)
                        nc.scalar.copy(partm[:, n, :], ropeb[:, n, :]).then_inc(act_split, 1)
                if k == 4:
                    if 0 <= it + 1 < B:
                        g = 2 * it + 2
                        take("MROW0", it + 1)
                        if g >= 2:
                            act.wait_ge(mrow_out[0], 16 * (g // 2))
                        nc.scalar.copy(mt[:, 0, :], miscb[:, 0:T]).then_inc(misc_free, 1)
                if k == 6 and 0 <= it - 1 < B:
                    take("YT", it - 1)
                    nc.scalar.copy(yt2[:, :], misc).then_inc(misc_free, 1)

            def experts(layer):
                base = GROUPS * layer
                pad(act, ENG.Activation, layer, NE // 2)
                if layer:
                    act.wait_ge(bank_ready[7], bjob["O3", B - 1][1] + 1)
                else:
                    act.wait_ge(misc_ready, job["Y3", B - 1] + 1)
                    act.wait_ge(ew_in, 16 * 8)
                act.wait_ge(tab_v, NTAB * (layer + 1))

                def step(s, u, rnd):
                    if layer or not isinstance(s, int) or s >= 2:
                        act.wait_ge(h_ready, s + (base - 1))
                    for i in range(G):
                        col = column_of(ENG.Activation, s * G + i)
                        cp = nc.scalar.copy(ktile[:, u % 2, P * i:P * i + P], kw[:, bass.ds(col, C)])
                    cp.then_inc(ktile_done, 1)

                expert_rounds(act, step, 0)

            def bank_take(name, b):
                bank, n = bjob[name, b]
                act.wait_ge(bank_ready[bank], n + 1)
                return ps[:, bank, :], bank_free[bank]

            def attention_b(name, b):
                o, free = bank_take(name, b) if name[0] != "E" else (None, None)
                i = int(name[1]) if name[0] in "EP" else 0
                if name == "XT":
                    if b:
                        act.wait_ge(bank_ready[3], b)
                    nc.scalar.copy(xnt[:, 0, :], o).then_inc(free, 1)
                elif name == "NT":
                    nc.scalar.copy(ntt[:, :], o).then_inc(free, 1)
                    n = B + b
                    act.wait_ge(sent[b % 2], 256 * (n // 2))
                    for t in range(TT):
                        nc.scalar.copy(xs[:, b % 2, t, :, 0:C],
                                       xn1[:, t, :].unsqueeze(1).broadcast_to([P, TOPK, C])).then_inc(xs_filled, 1)
                elif name == "Q":
                    if b:
                        act.wait_ge(bank_ready[5], bjob["S3", b - 1][1] + 1)
                    nc.scalar.copy(ropea[:, 0, :], o).then_inc(free, 1)
                elif name == "V":
                    if b:
                        act.wait_ge(bank_ready[7], bjob["O3", b - 1][1] + 1)
                    nc.scalar.copy(ropeb[:, 0, :], o).then_inc(free, 1)
                elif name == "LG":
                    act.wait_ge(top_seq, 11 * (B + b - 1) + 10)
                    nc.scalar.activation(sg[:, :, :].rearrange("p t e -> p (t e)"), o[:, 0:TT * NE], ACT.Exp,
                                         scale=-1.0).then_inc(free, 1)
                elif name[0] == "E":
                    n = TT * b + i
                    act.wait_ge(nrow_done, n + 1)
                    if n >= 2:
                        bank, k = bjob[f"P{(n - 2) % TT}", (n - 2) // TT]
                        act.wait_ge(bank_ready[bank], k + 1)
                    if n >= TT:
                        act.wait_ge(rinv_done, n - TT + 1)
                    nc.scalar.activation(probb[:, i % 2, :], masked[:, i % 2, :], ACT.Exp, bias=nrow[:, i:i + 1],
                                         scale=SCALE_B, accum_out=rowsum[:, i:i + 1]).then_inc(expb_done, 1)
                elif name[0] == "P":
                    n = TT * b + i
                    if n >= 2:
                        bank, k = bjob[f"O{(n - 2) % TT}", (n - 2) // TT]
                        act.wait_ge(bank_ready[bank], k + 1)
                    nc.scalar.copy(probt[:, i % 2, :], o).then_inc(free, 1)

            experts(0)
            for it in range(LAST_IT_B + 1):
                for name, off in (("XT", 0), ("NT", -1), ("Q", 0), ("V", 0), ("LG", -1), ("E0", 0), ("E1", 0), ("P0", 0),
                                  ("E2", 0), ("P1", 0), ("E3", 0), ("P2", 0), ("P3", 0)):
                    if 0 <= it + off < B:
                        attention_b(name, it + off)
            experts(1)

        @block.vector
        def _(dve):
            def take(name, b):
                dve.wait_ge(misc_ready, job[name, b] + 1)

            def ln_stats(src, st, mv, rs, b, seq):
                for t in range(TT):
                    nc.vector.bn_stats(st[:, t, :], src[:, t, :]).then_inc(seq, 1)
                dve.wait_ge(seq, 13 * b + 4)
                for t in range(TT):
                    nc.vector.bn_aggr(mv[:, t, :], st[:, t, :]).then_inc(seq, 1)
                dve.wait_ge(seq, 13 * b + 8)
                nc.vector.tensor_scalar(rs[:, :], mv[:, :, 1], EPS, None, ALU.add).then_inc(seq, 1)

            def ln_apply(src, mv, rs, dst, b, seq, rstd):
                dve.wait_ge(rstd, b + 1)
                for t in range(TT):
                    nc.vector.tensor_scalar(dst[:, t, :], src[:, t, :], mv[:, t, 0:1], rs[:, t:t + 1],
                                            ALU.subtract, ALU.mult).then_inc(seq, 1)

            def maxima(pr):
                p = pr % 4
                if p == 0 and pr:
                    dve.wait_ge(mrow_seq, 5 * (pr // 4 - 1) + 1)
                for u, parts in enumerate([[(0, 3, 0)], [(0, 0, 0), (0, 2, 128)], [(1, 3, 0)], [(1, 0, 0), (1, 2, 128)]]):
                    n = 5 * pr + u
                    dve.wait_ge(s1_ready, n + 1)
                    for hb, i, at in parts:
                        red = nc.vector.tensor_reduce(mx[:, i, 2 * p + hb:2 * p + hb + 1],
                                                      ps[:, 4 + n % 2, at:at + P * (i + 1)], AX.X, ALU.max)
                    red.then_inc(s1_free, 1)
                n = 5 * pr + 4
                dve.wait_ge(s1_ready, n + 1)
                nc.vector.tensor_reduce(mx[:, 1, 2 * p:2 * p + 2], ps[:, 4 + n % 2, :].rearrange("p (h n) -> p h n", h=2),
                                        AX.X, ALU.max).then_inc(s1_free, 1)

            def max_parts(g):
                dve.wait_ge(s1_free, 20 * g + 20)
                nc.vector.tensor_scalar(mneg[:, :, :], mx[:, :, :], -1.0, None, ALU.mult).then_inc(mrow_seq, 1)
                dve.wait_ge(mrow_seq, 5 * g + 1)
                if g:
                    dve.wait_ge(misc_ready, job["MROW0" if g % 2 else "MROW1", (g - 1) // 2] + 1)
                nc.vector.tensor_copy(mparts[:, :, :, 0], mneg[:, :, :]).then_inc(mrow_seq, 1)
                dve.wait_ge(mrow_seq, 5 * g + 2)
                nc.vector.tensor_tensor(mres[:, :, :], mneg[:, :, :], mparts[:, :, :, 0], ALU.subtract).then_inc(mrow_seq, 1)
                dve.wait_ge(mrow_seq, 5 * g + 3)
                nc.vector.tensor_copy(mparts[:, :, :, 1], mres[:, :, :]).then_inc(mrow_seq, 1)
                dve.wait_ge(mrow_seq, 5 * g + 4)
                nc.vector.tensor_tensor(mparts[:, :, :, 2], mres[:, :, :], mparts[:, :, :, 1], ALU.subtract).then_inc(mrow_seq, 1)

            def rotate_weights():
                for n in range(2):
                    at = 6 * n
                    for m in range(2):
                        nc.vector.tensor_tensor(wrot[:, m, :], w[:, C * (2 * n + m):C * (2 * n + m + 1)], trig_row[:, m, :],
                                                ALU.mult).then_inc(rotated, 1)
                    dve.wait_ge(rotated, at + 2)
                    nc.vector.tensor_tensor(wqk[:, n, :], wrot[:, 0, :], wrot[:, 1, :], ALU.add).then_inc(rotated, 1)
                    for m in range(2):
                        nc.vector.tensor_tensor(brot[:, m:m + 1], bcol[:, 2 * n + m:2 * n + m + 1], trig_col[:, m:m + 1],
                                                ALU.mult).then_inc(rotated, 1)
                    dve.wait_ge(rotated, at + 5)
                    nc.vector.tensor_tensor(bqk[:, n:n + 1], brot[:, 0:1], brot[:, 1:2], ALU.add).then_inc(rotated, 1)
                    dve.wait_ge(rotated, at + 6)

            def add_bias(name, b):
                n = "QK".index(name)
                take(name, b)
                if b:
                    dve.wait_ge(pool_split, 4 * b)
                nc.vector.tensor_scalar(ropea[:, n, :], misc, bqk[:, n:n + 1], None, ALU.add).then_inc(misc_free, 1)

            def head_outputs(i, b):
                take(f"Y{i}", b)
                m = misc.rearrange("p (h d) -> p h d", h=NH)
                if i or b:
                    dve.wait_ge(misc_free, job[f"Y{i}", b])
                nc.vector.reciprocal(yrc[:, :], m[:, :, HD]).then_inc(yrc_done, 1)
                dve.wait_ge(yrc_done, 4 * b + i + 1)
                nc.vector.tensor_tensor(ytok[:, i, :].rearrange("p (h d) -> p h d", h=NH), m[:, :, 0:HD],
                                        yrc[:, :].unsqueeze(2).broadcast_to([P, NH, HD]), ALU.mult).then_inc(misc_free, 1)

            def choose(b, exp_done_sem, exp_done_n):
                dve.wait_ge(exp_done_sem, exp_done_n)
                if b:
                    dve.wait_ge(top_seq, 11 * b)
                nc.vector.tensor_scalar(sg[:, :, :], sg[:, :, :], 1.0, None, ALU.add).then_inc(top_seq, 1)
                dve.wait_ge(top_seq, 11 * b + 1)
                nc.vector.reciprocal(sg[:, :, :], sg[:, :, :]).then_inc(top_seq, 1)
                dve.wait_ge(top_seq, 11 * b + 2)
                for t in range(TT):
                    nc.vector.max(top[:, TT * (b % B) + t, :], sg[:, t, :]).then_inc(top_seq, 1)
                for t in range(TT):
                    dve.wait_ge(top_seq, 11 * b + 3 + t)
                    nc.vector.max_index(idx8[:, t, :], top[:, TT * (b % B) + t, :], sg[:, t, :]).then_inc(top_seq, 1)
                dve.wait_ge(top_seq, 11 * b + 10)
                nc.vector.tensor_copy(idxf[:, :, :], idx8[:, :, 0:TOPK]).then_inc(top_seq, 1)
                dve.wait_ge(top_seq, 11 * b + 11)
                if b:
                    dve.wait_ge(prod_done, b)
                nc.vector.tensor_tensor(oh[:, :, :, :].rearrange("p t s e -> p (t s) e"),
                                        iota_e[:, :].unsqueeze(1).broadcast_to([P, TT * TOPK, NE]),
                                        idxf[:, :, :].rearrange("p t s -> p (t s)").unsqueeze(2).broadcast_to([P, TT * TOPK, NE]),
                                        ALU.is_equal).then_inc(oh_done, 1)

            def chosen(b, rank_sem, rank_n):
                dve.wait_ge(oh_done, b + 1)
                if b:
                    dve.wait_ge(rank_sem, rank_n)
                with nc.allow_low_precision(reason="0 and 1 are exact"):
                    nc.vector.tensor_reduce(msum[:, :, :], oh[:, :, :, :].rearrange("p t s e -> p t e s"), AX.X,
                                            ALU.add).then_inc(msum_done, 1)

            def positions(b, bank, free):
                layer = b // B
                if b:
                    dve.wait_ge(prod_done, b)
                nc.vector.tensor_tensor(rpos[:, :, :], bank[:, 0:TT * NE].rearrange("p (t e) -> p t e", t=TT),
                                        ebase[:, :].unsqueeze(1).broadcast_to([P, TT, NE]), ALU.add).then_inc(free, 1)
                with nc.allow_low_precision(reason="counts up to 32 are exact"):
                    nc.vector.tensor_reduce(tsum[:, :], msum[:, :, :].rearrange("p t e -> p e t"), AX.X,
                                            ALU.add).then_inc(acc_seq, 1)
                dve.wait_ge(acc_seq, 2 * b + 1)
                nc.vector.tensor_tensor(acc[:, layer, :], acc[:, layer, :], tsum[:, :], ALU.add).then_inc(acc_seq, 1)

            def destinations(b):
                dve.wait_ge(prod_done, b + 1)
                if b:
                    dve.wait_ge(dest_seq, 2 * b)
                nc.vector.tensor_reduce(destf[:, :], prod[:, :, :, :].rearrange("p t s e -> p (t s) e"), AX.X,
                                        ALU.add).then_inc(dest_seq, 1)
                dve.wait_ge(dest_seq, 2 * b + 1)
                nc.vector.tensor_copy(dest[:, 16 * (b % B):16 * (b % B) + 16], destf[:, :]).then_inc(dest_seq, 1)

            nc.vector.memset(czero, 0.0).then_inc(consts_v, 1)
            nc.vector.memset(cone, 1.0).then_inc(consts_v, 1)
            nc.vector.memset(mhalf[:, :], -0.5).then_inc(consts_v, 1)
            nc.vector.memset(acc[:, :, :], 0.0).then_inc(consts_v, 1)
            nc.vector.memset(mparts[:, :, :, 3], 0.0).then_inc(consts_v, 1)
            nc.vector.memset(kz[64:128, :, 0, :, :], 0.0).then_inc(consts_v, 1)
            nc.vector.memset(kz[0:64, :, 1, :, :], 0.0).then_inc(consts_v, 1)
            nc.vector.memset(vaug[:, :, :, :, HD + 1:32], 0.0).then_inc(consts_v, 1)
            nc.vector.memset(vaug[:, :, :, :, HD:HD + 1], 1.0).then_inc(consts_v, 1)
            dve.wait_ge(in_w, 16 * 9)
            dve.wait_ge(in_x, 32)
            dve.wait_ge(consts, NCONST)
            rotate_weights()
            for it, k in slots():
                pr = 8 * it + k + NP
                if 0 <= pr < B * NP:
                    maxima(pr)
                    if pr % 4 == 3:
                        max_parts(pr // 4)
                pre, post, last, nxt = it + 2, it - 1, it - 2, it + 3
                if k == 0 and 0 <= last < B:
                    if last:
                        dve.wait_ge(xs_filled, TT * last)
                    ln_apply(x[:, TT * last:TT * last + TT, :], mv1, rs1, xn1, last, ln1, rstd1)
                if k == 4 and 0 <= nxt < B:
                    ln_stats(x[:, TT * nxt:TT * nxt + TT, :], st0, mv0, rs0, nxt, ln0)
                if k == 6 and 0 <= nxt < B:
                    if nxt:
                        dve.wait_ge(misc_ready, job["XT", nxt - 1] + 1)
                    ln_apply(x[:, TT * nxt:TT * nxt + TT, :], mv0, rs0, xn0, nxt, ln0, rstd0)
                if k == 1:
                    if 0 <= pre < B:
                        add_bias("Q", pre)
                        add_bias("K", pre)
                if k == 2:
                    if 0 <= last < B:
                        choose(last, misc_free, job["LG", last] + 1)
                if k == 3:
                    if 0 <= last < B:
                        chosen(last, misc_ready, job["RK", last - 1] + 1 if last else 0)
                    if 0 <= it + 1 < B:
                        b = it + 1
                        take("V", b)
                        if b >= 2:
                            dve.wait_ge(pv_done, 4 * (b - 2) + 4)
                        nc.vector.tensor_tensor(
                            vaug[:, b % 2, :, :, 0:HD], misc.rearrange("p (t h d) -> p t h d", t=TT, h=NH),
                            bv[:, :].rearrange("p (h d) -> p h d", h=NH).unsqueeze(1).broadcast_to([P, TT, NH, HD]),
                            ALU.add).then_inc(misc_free, 1)
                    if 0 <= post < B:
                        head_outputs(0, post)
                if k == 4:
                    if 0 <= last < B:
                        take("RK", last)
                        positions(last, misc, misc_free)
                    if 0 <= post < B:
                        head_outputs(1, post)
                if k == 5:
                    if 0 <= post < B:
                        head_outputs(2, post)
                        head_outputs(3, post)
                if k == 6 and 0 <= last < B:
                    destinations(last)
                if k == 7:
                    if 0 <= post < B:
                        b = post
                        take("PJ", b)
                        dve.wait_ge(xb_done, b + 1)
                        nc.vector.tensor_tensor(x[:, TT * b:TT * b + TT, :], misc.rearrange("p (t c) -> p t c", t=TT),
                                                x[:, TT * b:TT * b + TT, :], ALU.add).then_inc(misc_free, 1)
                        dve.wait_ge(misc_free, job["PJ", b] + 1)
                        ln_stats(x[:, TT * b:TT * b + TT, :], st1, mv1, rs1, b, ln1)


            def tile_table(layer):
                bank = ps[:, 6, :]
                v, q = NTAB * layer, 3 * layer
                dve.wait_ge(tab_pe, q + 1)
                nc.vector.tensor_copy(count[:, :], bank[0:NE, 0:1]).then_inc(tab_v, 1)
                dve.wait_ge(tab_v, v + 1)
                nc.vector.tensor_tensor(padrow[:, :], bank[0:1, 384:384 + NE], ebase[0:1, :], ALU.add).then_inc(tab_v, 1)
                nc.vector.tensor_scalar(ceil_i[:, :], count[:, :], float(P - 1), None, ALU.add).then_inc(tab_v, 1)
                dve.wait_ge(tab_v, v + 3)
                nc.vector.tensor_scalar(ceil_s[:, :], ceil_i[:, :], 7, None, ALU.arith_shift_right).then_inc(tab_v, 1)
                dve.wait_ge(tab_v, v + 4)
                nc.vector.tensor_copy(ntile[:, :], ceil_s[:, :]).then_inc(tab_v, 1)
                dve.wait_ge(tab_v, v + 5)
                nc.vector.tensor_scalar(skip[:, :], ntile[:, :], -1.0, float(REGION // P), ALU.mult, ALU.add).then_inc(tab_v, 1)
                dve.wait_ge(tab_pe, q + 2)
                nc.vector.tensor_copy(upto[:, :], bank[0:NE, 0:1]).then_inc(tab_v, 1)
                dve.wait_ge(tab_v, v + 7)
                nc.vector.tensor_scalar(past, iota_t[:, :], upto[:, 0:1], None, ALU.is_ge).then_inc(tab_v, 1)
                dve.wait_ge(tab_pe, q + 3)
                nc.vector.tensor_scalar(tile_e, bank[0:1, 0:NTILES], float(NE - 1), float(C), ALU.min,
                                        ALU.mult).then_inc(tab_v, 1)
                nc.vector.tensor_tensor(rowf, bank[0:1, NTILES:2 * NTILES], iota_t[0:1, :], ALU.add).then_inc(tab_v, 1)
                dve.wait_ge(tab_v, v + 10)
                nc.vector.tensor_scalar(tile_r, rowf, float(DUMMY), float(P), ALU.min, ALU.mult).then_inc(tab_v, 1)

            def experts(layer):
                base = GROUPS * layer
                if layer:
                    dve.wait_ge(bank_ready[7], bjob["O3", B - 1][1] + 1)
                    dve.wait_ge(combined, 16 * B)
                else:
                    dve.wait_ge(misc_ready, job["Y3", B - 1] + 1)
                    dve.wait_ge(pv_done, 4 * B)

                def step(s, u, rnd):
                    static = isinstance(s, int)
                    if not static or s < GROUPS:
                        dve.wait_ge(t1_ready, s + (base + 1))
                        if layer or not static or s >= 2:
                            dve.wait_ge(h_ready, s + (base - 1))
                        nc.vector.tensor_copy(xtt[:, u % 2, :], ps[:, u % 2, :]).then_inc(t1_done, 1)
                    if not static or 1 <= s < GROUPS + 1:
                        v = (u + 1) % 2
                        dve.wait_ge(h_ready, s + base)
                        if layer or not static or s >= 3:
                            dve.wait_ge(y_ready, s + (base - 2))
                        nc.vector.tensor_scalar(hidt[:, v, :], ps[:, 2 + v, :], 0.0, None, ALU.max).then_inc(h_done, 1)
                    if not static or s >= 2:
                        v, q = u % 2, (u - 2) % U
                        dve.wait_ge(y_ready, s + (base - 1))
                        done = rnd + (ROUNDS * layer if u >= 2 else ROUNDS * layer - 1)
                        if not isinstance(done, int) or done > 0:
                            dve.wait_ge(y_sent[q], done * (16 * G))
                        nc.vector.tensor_copy(yout[:, G * q:G * q + G, :],
                                              ps[:, 4 + v, :].rearrange("p (g n) -> p g n", g=G)).then_inc(y_done, 1)

                expert_rounds(dve, step, 2, 2)

            def combine(layer, b):
                n = B * layer + b
                dve.wait_ge(yg_in[b % 2], 16 * (n // 2 + 1))
                for c in range(TOPK):
                    dve.wait_ge(combined, 16 * n + TT * c)
                    for t in range(TT):
                        xt = x[:, TT * b + t, :]
                        nc.vector.scalar_tensor_tensor(out=xt, in0=yg[:, b % 2, t, C * c:C * c + C],
                                                       scalar=top[:, TT * b + t, c:c + 1], in1=xt,
                                                       op0=ALU.mult, op1=ALU.add).then_inc(combined, 1)

            def bank_take(name, b):
                bank, n = bjob[name, b]
                dve.wait_ge(bank_ready[bank], n + 1)
                return ps[:, bank, :], bank_free[bank]

            def score_rows(i, b):
                n = TT * b + i
                o, free = bank_take(f"S{i}", b)
                if n >= 2:
                    dve.wait_ge(expb_done, n - 1)
                nc.vector.tensor_tensor_reduce(out=masked[:, i % 2, :], in0=o, in1=band[:, i, :], scale=1.0,
                                               scalar=-3.0e38, op0=ALU.mult, op1=ALU.max,
                                               accum_out=rowmax[:, i:i + 1]).then_inc(free, 1)
                bank, k = bjob[f"S{i}", b]
                dve.wait_ge(bank_free[bank], k + 1)
                nc.vector.tensor_scalar(nrow[:, i:i + 1], rowmax[:, i:i + 1], -SCALE_B, None, ALU.mult).then_inc(nrow_done, 1)

            def score_out(i, b):
                n = TT * b + i
                dve.wait_ge(expb_done, n + 1)
                nc.vector.reciprocal(rinv[:, i:i + 1], rowsum[:, i:i + 1]).then_inc(rinv_done, 1)
                dve.wait_ge(rinv_done, n + 1)
                o, free = bank_take(f"O{i}", b)
                xt = x[:, TT * b + i, :]
                nc.vector.scalar_tensor_tensor(out=xt, in0=o[:, 0:C], scalar=rinv[:, i:i + 1], in1=xt,
                                               op0=ALU.mult, op1=ALU.add).then_inc(free, 1)

            def combine_and_norm(b):
                combine(0, b)
                dve.wait_ge(combined, 16 * b + 16)
                ln_stats(x[:, TT * b:TT * b + TT, :], st0, mv0, rs0, b, ln2)
                if b:
                    dve.wait_ge(bank_ready[0], bjob["XT", b - 1][1] + 1)
                ln_apply(x[:, TT * b:TT * b + TT, :], mv0, rs0, xn0, b, ln2, rstd2)

            tile_table(0)
            experts(0)
            dve.wait_ge(band_made, 3)
            combine_and_norm(0)
            for b in range(LAST_IT_B + 1):
                r = b - 1
                front, route = b < B, 0 <= r < B
                if route:
                    dve.wait_ge(xs_filled, TT * (B + r))
                    ln_apply(x[:, TT * r:TT * r + TT, :], mv1, rs1, xn1, r, ln3, rstd3)
                if front:
                    o, free = bank_take("K", b)
                    if b:
                        dve.wait_ge(bank_ready[5], bjob["S3", b - 1][1] + 1)
                    nc.vector.tensor_copy(ropea[:, 1, :], o).then_inc(free, 1)
                    score_rows(0, b)
                    score_rows(1, b)
                if route:
                    bank, n = bjob["LG", r]
                    choose(B + r, bank_free[bank], n + 1)
                    if r:
                        bank, n = bjob["RK", r - 1]
                        chosen(B + r, bank_ready[bank], n + 1)
                    else:
                        chosen(B, misc_ready, len(job))
                if front:
                    score_out(0, b)
                    score_rows(2, b)
                    score_out(1, b)
                if route:
                    o, free = bank_take("RK", r)
                    positions(B + r, o, free)
                if front:
                    score_rows(3, b)
                    score_out(2, b)
                    score_out(3, b)
                    dve.wait_ge(bank_free[7], bjob["O3", b][1] + 1)
                    if b:
                        dve.wait_ge(ln3, 13 * b)
                    ln_stats(x[:, TT * b:TT * b + TT, :], st1, mv1, rs1, b, ln3)
                if route:
                    if r == 0:
                        for i in range(2):
                            dve.wait_ge(sent[i], 256 * (B // 2))
                    destinations(B + r)
                if b + 1 < B:
                    combine_and_norm(b + 1)
            tile_table(1)
            experts(1)
            for b in range(B):
                combine(1, b)

        @block.gpsimd
        def _(pool):
            g = nc.gpsimd
            g.memset(ident[:, :], 0.0).then_inc(consts, 1)
            g.memset(maskneg[:, :], 0.0).then_inc(consts, 1)
            g.memset(onesb[:, :], 1.0).then_inc(consts, 1)
            g.memset(xs[:, :, :, :, C + 1:ROW], 0.0).then_inc(consts, 1)
            g.iota(iota_e[:, :], pattern=[[1, NE]], base=0, channel_multiplier=0,
                   allow_small_or_imprecise_dtypes=True).then_inc(consts, 1)
            g.iota(ebase[:, :], pattern=[[REGION, NE]], base=0, channel_multiplier=0,
                   allow_small_or_imprecise_dtypes=True).then_inc(consts, 1)
            pool.wait_ge(consts, 6)
            g.affine_select(out=ident[:, :], in_=ident[:, :], compare_op=ALU.not_equal, fill=1.0, base=0,
                            pattern=[[-1, P]], channel_multiplier=1).then_inc(consts, 1)
            g.affine_select(out=maskneg[:, :], in_=maskneg[:, :], compare_op=ALU.is_ge, fill=NEG, base=0,
                            pattern=[[-1, P]], channel_multiplier=1)
            g.affine_select(out=tri[:, :], in_=onesb[:, :], compare_op=ALU.is_gt, fill=0.0, base=0,
                            pattern=[[1, P]], channel_multiplier=-1).then_inc(consts, 1)
            g.affine_select(out=trii[:, :], in_=onesb[:, :], compare_op=ALU.is_ge, fill=0.0, base=0,
                            pattern=[[1, P]], channel_multiplier=-1).then_inc(consts, 1)
            g.iota(iota_t[:, :], pattern=[[1, NTILES]], base=0, channel_multiplier=0,
                   allow_small_or_imprecise_dtypes=True).then_inc(consts, 1)
            pool.wait_ge(consts, 7)
            g.tensor_copy(identb[:, :], ident[:, :]).then_inc(consts, 1)

            pool.wait_ge(in_w, 16 * 9)
            pool.wait_ge(consts_v, NCONSTV)
            for it, k in slots():
                if k == 0 and 0 <= it - 2 < B:
                    pool.wait_ge(ln1, 13 * (it - 2) + 9)
                    g.tensor_tensor(rs1[:, :], rs1[:, :], mhalf[:, :], ALU.pow).then_inc(rstd1, 1)
                if k == 5 and 0 <= it + 3 < B:
                    pool.wait_ge(ln0, 13 * (it + 3) + 9)
                    g.tensor_tensor(rs0[:, :], rs0[:, :], mhalf[:, :], ALU.pow).then_inc(rstd0, 1)
                pr = 8 * it + k
                if 0 <= pr < B * NP:
                    pool.wait_ge(exp_done, 3 * pr + 3)
                    pb = prob[:, (pr // 2) % 2, pr % 2, :]
                    for lo, hi, n in ((0, 2048, 4), (2048, 2560, 2)):
                        v = pb[:, lo:hi].rearrange("p (a n) -> p a n", a=n)[:, :, 0:P]
                        g.affine_select(out=v, in_=v, compare_op=ALU.is_ge, fill=0.0, base=0,
                                        pattern=[[0, n], [1, P]], channel_multiplier=-1)
                    v = pb[:, 0:2048].rearrange("p (a n) -> p a n", a=2)[:, :, 896:1024]
                    g.affine_select(out=v, in_=v, compare_op=ALU.is_ge, fill=0.0, base=0,
                                    pattern=[[0, 2], [1, P]], channel_multiplier=-1).then_inc(sel_done, 1)
                b = it + 2
                if 0 <= b < B:
                    if k == 0:
                        pool.wait_ge(ln0, 13 * b + 13)
                        xb = x[:, TT * b:TT * b + TT, :]
                        g.tensor_tensor(xb, xb, bproj[:, :].unsqueeze(1).broadcast_to([P, TT, C]), ALU.add).then_inc(xb_done, 1)
                    if k == 2:
                        for n in range(2):
                            pool.wait_ge(act_split, 4 * b + n + 1)
                            g.tensor_tensor(ropeb[:, n, :], ropea[:, n, :], parth[:, n, :], ALU.subtract).then_inc(pool_split, 1)
                    if k == 3:
                        for n in range(2):
                            pool.wait_ge(act_split, 4 * b + n + 3)
                            g.tensor_tensor(partl[:, n, :], ropeb[:, n, :], partm[:, n, :], ALU.subtract).then_inc(pool_split, 1)
                b = it - 2
                if 0 <= b < B:
                    if k == 1:
                        if b >= 2:
                            pool.wait_ge(sent[b % 2], 256 * (b // 2))
                        g.iota(xs[:, b % 2, :, :, C:C + 1].bitcast(I32).rearrange("p t s o -> p t (s o)"),
                               pattern=[[TOPK * P, TT], [1, TOPK]], base=TOPK * T * b,
                               channel_multiplier=TOPK).then_inc(meta_done, 1)
                    if k == 5:
                        pool.wait_ge(misc_free, job["RK", b] + 1)
                        if b:
                            pool.wait_ge(dest_seq, 2 * b)
                        g.tensor_tensor(prod[:, :, :, :], oh[:, :, :, :],
                                        rpos[:, :, :].unsqueeze(2).broadcast_to([P, TT, TOPK, NE]), ALU.mult).then_inc(prod_done, 1)
                b, c = scatter_chunk(it, k)
                if 0 <= b < B:
                    if c == 0:
                        pool.wait_ge(dest_seq, 2 * b + 2)
                        pool.wait_ge(xs_filled, TT * b + TT)
                        pool.wait_ge(meta_done, b + 1)
                    for n in (2 * c, 2 * c + 1):
                        g.indirect_dma_start(sorted_d[0][:, :], bass.IndirectOffsetOnAxis(dest[:, 16 * b + n:16 * b + n + 1], 0),
                                             xs[:, b % 2, n // TOPK, n % TOPK, :], None).then_inc(sent[b % 2], 16)


            pool.wait_ge(s2_ready, 3 * B * NP)
            pool.wait_ge(s1_ready, 5 * B * NP)
            g.memset(pads, 0.0).then_inc(pads_made, 1)
            pool.wait_ge(pads_made, 1)
            g.iota(pads.bitcast(I32).rearrange("p (r n) -> p r n", n=ROW)[:, :, C], pattern=[[0, 4]], base=NOWHERE,
                   channel_multiplier=0).then_inc(pads_made, 1)

            last_result = pool.to_reg(ROWS - 1)

            def experts(layer):
                base = GROUPS * layer

                def send(s, u, rnd):
                    pool.wait_ge(y_done, s + (base + 1))
                    g.nop(nofuse=True)
                    for i in range(G * u, G * u + G):
                        g.indirect_dma_start(result_d[layer][:, :], bass.IndirectOffsetOnAxis(xin[:, i, C:C + 1].bitcast(I32), 0),
                                             yout[:, i, :], None, bounds_check=last_result, oob_is_err=False).then_inc(y_sent[u], 16)

                expert_rounds(pool, send, 0)

            def scatters(b, half):
                for n in range(8 * half, 8 * half + 8):
                    g.indirect_dma_start(sorted_d[1][:, :], bass.IndirectOffsetOnAxis(dest[:, 16 * b + n:16 * b + n + 1], 0),
                                         xs[:, b % 2, n // TOPK, n % TOPK, :], None).then_inc(sent[b % 2], 16)

            g.memset(band, 1.0).then_inc(band_made, 1)
            pool.wait_ge(band_made, 1)
            g.affine_select(out=band, in_=band, compare_op=ALU.is_ge, fill=0.0, base=32,
                            pattern=[[-P, TT], [1, T]], channel_multiplier=-1).then_inc(band_made, 1)
            pool.wait_ge(band_made, 2)
            g.affine_select(out=band, in_=band, compare_op=ALU.is_ge, fill=0.0, base=31,
                            pattern=[[P, TT], [-1, T]], channel_multiplier=1).then_inc(band_made, 1)
            experts(0)
            for u in range(U):
                pool.wait_ge(y_sent[u], 16 * G * ROUNDS)
            g.memset(xs[:, :, :, :, C + 1:ROW], 0.0).then_inc(pads_made, 1)
            pool.wait_ge(ln2, 9)
            g.tensor_tensor(rs0[:, :], rs0[:, :], mhalf[:, :], ALU.pow).then_inc(rstd2, 1)
            for b in range(LAST_IT_B + 1):
                r = b - 1
                if 0 <= r < B:
                    pool.wait_ge(ln3, 13 * r + 9)
                    g.tensor_tensor(rs1[:, :], rs1[:, :], mhalf[:, :], ALU.pow).then_inc(rstd3, 1)
                    pool.wait_ge(sent[r % 2], 256 * ((B + r) // 2))
                    g.iota(xs[:, r % 2, :, :, C:C + 1].bitcast(I32).rearrange("p t s o -> p t (s o)"),
                           pattern=[[TOPK * P, TT], [1, TOPK]], base=TOPK * T * r,
                           channel_multiplier=TOPK).then_inc(meta_done, 1)
                if 0 <= r - 1 < B:
                    scatters(r - 1, 1)
                if 0 <= r < B:
                    bank, n = bjob["RK", r]
                    pool.wait_ge(bank_free[bank], n + 1)
                    pool.wait_ge(dest_seq, 2 * (B + r))
                    g.tensor_tensor(prod[:, :, :, :], oh[:, :, :, :],
                                    rpos[:, :, :].unsqueeze(2).broadcast_to([P, TT, TOPK, NE]), ALU.mult).then_inc(prod_done, 1)
                if b + 1 < B:
                    pool.wait_ge(ln2, 13 * (b + 1) + 9)
                    g.tensor_tensor(rs0[:, :], rs0[:, :], mhalf[:, :], ALU.pow).then_inc(rstd2, 1)
                if 0 <= r < B:
                    pool.wait_ge(dest_seq, 2 * (B + r) + 2)
                    pool.wait_ge(xs_filled, TT * (B + r) + TT)
                    pool.wait_ge(meta_done, B + r + 1)
                    pool.wait_ge(pads_made, 3)
                    scatters(r, 0)
            experts(1)


def kernel(**inputs):
    import numpy as np
    import concourse.bacc as bacc
    from concourse.bass_utils import run_bass_kernel_spmd

    a = {k: np.ascontiguousarray(v) for k, v in inputs.items()}
    swap = np.arange(C) ^ 1
    wa, ba = a["L0_attn_a_W_attn"], a["L0_attn_a_b_attn"]
    theta = (1.0 / np.float32(10000.0) ** (np.arange(0, HD, 2, dtype=np.float32) / np.float32(HD))).astype(np.float32)
    angle = (np.arange(C) // HD).astype(np.float32) * theta[(np.arange(C) % HD) // 2]
    sign = np.where(np.arange(C) % 2 == 0, -1.0, 1.0).astype(np.float32)
    trig = np.stack([np.cos(angle), np.sin(angle) * sign]).astype(np.float32)
    arrays = {
        "x": a["L0_attn_a_x"].reshape(B * T, C),
        "w": np.concatenate([wa[:, 0:C], wa[:, 0:C][:, swap], wa[:, C:2 * C], wa[:, C:2 * C][:, swap], wa[:, 2 * C:]], axis=1),
        "bcol": np.stack([ba[0:C], ba[0:C][swap], ba[C:2 * C], ba[C:2 * C][swap]], axis=1),
        "bv": ba[2 * C:],
        "wproj": a["L0_attn_a_W_proj"],
        "bproj": a["L0_attn_a_b_proj"],
        "trig_row": trig.reshape(2 * C),
        "trig_col": trig.T,
        "wb": np.concatenate([a["L0_attn_b_WQ"], a["L0_attn_b_WK"], a["L0_attn_b_WV"]], axis=1),
        "esel": a["L0_ffn_expert_sel"].T,
        "keys": a["L0_ffn_keys"],
        "values": a["L0_ffn_values"],
    }
    arrays = {f"in_{k}": np.ascontiguousarray(v) for k, v in arrays.items()}
    nc = bacc.Bacc("TRN2", target_bir_lowering=False, num_devices=1)
    args = [nc.dram_tensor(k, v.shape, F32, kind="ExternalInput").ap() for k, v in arrays.items()]
    out = nc.dram_tensor("out", (B * T, C), F32, kind="ExternalOutput").ap()
    build(nc, *args, out)
    r = run_bass_kernel_spmd(nc, [arrays], core_ids=[0])
    return r.results[0]["out"].reshape(B, T, C)
```

```python
from contextlib import ExitStack

import concourse.bass as bass
from concourse import mybir

F32 = mybir.dt.float32
BF16 = mybir.dt.bfloat16
I32 = mybir.dt.int32
U32 = mybir.dt.uint32
ALU = mybir.AluOpType
ACT = mybir.ActivationFunctionType
AX = mybir.AxisListType
ENG = mybir.EngineType

P = 128
B, T, C = 8, 512, 128
TT = T // P
NT = B * TT
NH, HD = 16, 8
NP = NH // 2
NE, TOPK = 64, 4
ROWS = B * T * TOPK
REGION = B * T + P
ROW = C + 4
NTILES = (ROWS - NE) // P + NE + 1
NTILES += -NTILES % 32
DUMMY = NE * REGION // P
NOWHERE = 1 << 20
EPS = 1e-5
SCALE_A = float(HD) ** -0.5
SCALE_B = float(C) ** -0.5
NEG = -1e30

JOBS = [
    (0, 1, "MROW1", 0), (0, 2, "XT", 2),
    (1, 1, "NT", -2), (1, 2, "Q", 2), (1, 3, "K", 2),
    (2, 2, "LG", -2),
    (3, 1, "V", 1), (3, 3, "Y0", -1),
    (4, 1, "MROW0", 1), (4, 2, "RK", -2), (4, 3, "Y1", -1),
    (5, 1, "Y2", -1), (5, 3, "Y3", -1),
    (6, 2, "YT", -1),
    (7, 2, "PJ", -1),
]
FIRST_IT, LAST_IT = -3, B + 2


def job_numbers():
    n, out = 0, {}
    for it in range(FIRST_IT, LAST_IT + 1):
        for _, _, name, off in JOBS:
            if 0 <= it + off < B:
                out[name, it + off] = n
                n += 1
    return out


BJOBS = [(4, "S0", 0), (5, "S1", 0), (0, "NT", -1), (6, "P0", 0), (7, "O0", 0), (4, "S2", 0), (0, "XT", 1),
         (6, "P1", 0), (7, "O1", 0), (5, "S3", 0), (1, "LG", -1), (1, "Q", 1), (2, "K", 1), (6, "P2", 0), (7, "O2", 0),
         (3, "V", 1), (2, "RK", -1), (6, "P3", 0), (7, "O3", 0)]
LAST_IT_B = B + 1
G = 4
U = 8
ROUNDS = NTILES // (G * U)
GROUPS = NTILES // G


def bank_numbers():
    n, out = [0] * 8, {}
    for it in range(-1, LAST_IT_B + 1):
        for bank, name, off in BJOBS:
            if 0 <= it + off < B:
                out[name, it + off] = bank, n[bank]
                n[bank] += 1
    return out


QK_UNITS = [[(0, 3, 0)], [(0, 0, 0), (0, 2, 128)], [(1, 3, 0)], [(1, 0, 0), (1, 2, 128)], [(0, 1, 0), (1, 1, 256)]]

KQ_UNITS = [[(0, 0, 0)], [(0, 1, 0), (0, 3, 384)], [(1, 0, 0)], [(1, 1, 0), (1, 3, 384)], [(0, 2, 0), (1, 2, 256)]]


def slots():
    for it in range(FIRST_IT, LAST_IT + 1):
        for k in range(8):
            yield it, k


def build(nc, x_d, w_d, bcol_d, bv_d, wproj_d, bproj_d, trig_row_d, trig_col_d, wqkv_b_d, esel_d, keys_d, values_d, out_d):
    job = job_numbers()
    bjob = bank_numbers()
    with ExitStack() as ctx:
        def sb(name, shape, dt=F32):
            return ctx.enter_context(nc.sbuf_tensor(name, shape, dt))

        def sem(name):
            return ctx.enter_context(nc.semaphore(name))

        qd = nc.dram_tensor("q_parts", [2, NH, 64, T], BF16).ap()
        kd = nc.dram_tensor("k_parts", [2, NH, 64, T], BF16).ap()
        md = nc.dram_tensor("max_rows", [4, 32, T], BF16).ap()
        sorted_d = [nc.dram_tensor(f"sorted_rows{l}", [NE * REGION + P, ROW], F32).ap() for l in range(2)]
        result_d = [nc.dram_tensor(f"result_rows{l}", [ROWS, C], F32).ap() for l in range(2)]

        x = sb("x_res", [P, NT, C])
        arena = sb("arena", [P, 22528])
        prob = arena[:, 0:10240].rearrange("p (g r n) -> p g r n", g=2, r=2)
        kw = arena[:, 0:8192]
        vw = arena[:, 8192:16384]
        pads = arena[0:32, 16384:16384 + 4 * ROW]
        band = arena[:, 20608:21632].bitcast(BF16).rearrange("p (t n) -> p t n", t=TT)
        qs = arena[:, 10240:14336].bitcast(BF16).rearrange("p (s r n) -> p s r n", s=4, r=4)
        kz = arena[:, 14336:22528].bitcast(BF16).rearrange("p (s h r n) -> p s h r n", s=4, h=2, r=4)
        vaug = sb("v_aug", [P, 2, TT, NH, 32])
        yts = sb("y_heads", [P, 2, 4, T])
        xs = sb("x_send", [P, 2, TT, TOPK, ROW])
        w = sb("w_attn", [P, 5 * C])
        wrot = sb("w_rotated", [P, 2, C])
        wqk = sb("w_qk", [P, 2, C])
        bcol = sb("b_cols", [P, 4])
        brot = sb("b_rotated", [P, 3])
        bqk = sb("b_qk", [P, 2])
        bv = sb("b_v", [P, C])
        wproj = sb("w_proj", [P, C])
        bproj = sb("b_proj", [P, C])
        trig_row = sb("trig_row", [P, 2, C])
        trig_col = sb("trig_col", [P, 2])
        wb = sb("w_b", [P, 3 * C])
        esel = sb("expert_sel", [P, NE])
        ident = sb("ident", [P, P])
        identb = sb("identb", [P, P], BF16)
        maskneg = sb("maskneg", [P, P], BF16)
        tri = sb("tri", [P, P], BF16)
        onesb = sb("onesb", [P, P], BF16)
        iota_e = sb("iota_e", [P, NE])
        ebase = sb("ebase", [P, NE])
        xn0 = sb("xn0", [P, TT, C])
        xn1 = sb("xn1", [P, TT, C])
        st0 = sb("st0", [P, TT, 6])
        mv0 = sb("mv0", [P, TT, 2])
        rs0 = sb("rs0", [P, TT])
        st1 = sb("st1", [P, TT, 6])
        mv1 = sb("mv1", [P, TT, 2])
        rs1 = sb("rs1", [P, TT])
        mhalf = sb("minus_half", [P, TT])
        xnt = sb("xnt", [P, 2, T])
        ropea = sb("rope_a", [P, 2, T])
        ropeb = sb("rope_b", [P, 2, T])
        parth = sb("part_h", [P, 2, T], BF16)
        partm = sb("part_m", [P, 2, T], BF16)
        partl = sb("part_l", [P, 2, T], BF16)
        czero, cone = parth[:, 0, :], partm[0:48, 0, :]
        mx = sb("row_max", [P, TT, 8])
        mneg = sb("row_neg", [P, TT, 8])
        mres = sb("row_rest", [P, TT, 8])
        mparts = sb("max_parts", [P, TT, 8, 4], BF16)
        mt = sb("max_t", [32, 2, T], BF16)
        yrc = sb("y_recip", [P, NH])
        ytok = sb("y_tok", [P, TT, C])
        yt2 = sb("y_t", [P, T])
        ntt = sb("xn1_t", [P, T])
        sg = sb("sigmoid", [P, TT, NE])
        top = sb("gates", [P, NT, 8])
        idx8 = sb("idx8", [P, TT, 8], U32)
        idxf = sb("idxf", [P, TT, TOPK])
        oh = sb("one_hot", [P, TT, TOPK, NE], BF16)
        msum = sb("chosen", [P, TT, NE], BF16)
        acc = sb("chosen_before", [P, 2, NE], BF16)
        tsum = sb("chosen_now", [P, NE], BF16)
        rpos = sb("rank_pos", [P, TT, NE])
        prod = sb("pos_prod", [P, TT, TOPK, NE])
        destf = sb("dest_f", [P, TT * TOPK])
        dest = sb("dest", [P, NT * TOPK], I32)
        trii = sb("tri_incl", [P, P], BF16)
        iota_t = sb("iota_tiles", [NE, NTILES])
        count = sb("count", [NE, 1])
        padrow = sb("pad_row", [1, NE], I32)
        ceil_i = sb("ceil_i", [NE, 1], I32)
        ceil_s = sb("ceil_s", [NE, 1], I32)
        ntile = sb("tiles_of", [NE, 1], BF16)
        skip = sb("skip_of", [NE, 1], BF16)
        upto = sb("tiles_upto", [NE, 1])
        rowf = w[0:1, 0:NTILES]
        tile_e = w[0:1, NTILES:2 * NTILES].bitcast(I32)
        tile_r = w[0:1, 2 * NTILES:3 * NTILES].bitcast(I32)
        past = trig_row[0:NE, 0, 0:NTILES // 2].bitcast(BF16)
        xsf = xs[:, :, :, :, :].rearrange("p b t s n -> p (b t s n)")
        xin = xsf[:, 0:U * G * ROW].rearrange("p (u n) -> p u n", u=U * G)
        yout = vaug[:, :, :, :, :].rearrange("p b t h d -> p (b t h d)")[:, 0:U * G * C].rearrange("p (u n) -> p u n", u=U * G)
        ytf = yts[:, :, :, :].rearrange("p b g n -> p (b g) n")
        xtt, ktile, hidt = ytf[:, 0:2, :], ytf[:, 2:4, :], ytf[:, 4:6, :]
        yg = vaug[:, :, :, :, :].rearrange("p b t h d -> p b t (h d)")
        masked = ytf[:, 0:2, :]
        probb = ytf[:, 2:4, :]
        probt = ytf[:, 4:6, :]
        qkv = ((ropea[:, 0, :], ropea[:, 1, :], ropeb[:, 0, :]), (ropeb[:, 1, :], ytf[:, 6, :], ytf[:, 7, :]))
        rowmax = sb("row_max_b", [P, TT])
        nrow = sb("neg_max_b", [P, TT])
        rowsum = sb("row_sum_b", [P, TT])
        rinv = sb("row_inv_b", [P, TT])

        ps = ctx.enter_context(nc.psum_tensor("ps", [P, 8, 512], F32))
        misc = ps[:, 7, :]
        miscb = ps[0:32, 7, :].bitcast(BF16)
        pv = ps[:, 6, :]

        in_x = sem("in_x")
        in_w = sem("in_w")
        consts = sem("consts")
        consts_v = sem("consts_v")
        rows_init = sem("rows_init")
        misc_ready = sem("misc_ready")
        misc_free = sem("misc_free")
        ln0 = sem("ln0")
        ln1 = sem("ln1")
        rotated = sem("rotated")
        rstd0 = sem("rstd0")
        rstd1 = sem("rstd1")
        xb_done = sem("xb_done")
        pool_split = sem("pool_split")
        act_split = sem("act_split")
        parts_out = sem("parts_out")
        qk_landed = [sem(f"qk_landed{i}") for i in range(4)]
        s1_ready = sem("s1_ready")
        s1_free = sem("s1_free")
        mrow_seq = sem("mrow_seq")
        mrow_out = [sem(f"mrow_out{i}") for i in range(2)]
        mrow_landed = [sem(f"mrow_landed{i}") for i in range(4)]
        s2_ready = sem("s2_ready")
        exp_done = sem("exp_done")
        sel_done = sem("sel_done")
        pv_done = sem("pv_done")
        pv_evac = sem("pv_evac")
        yrc_done = sem("yrc_done")
        xs_filled = sem("xs_filled")
        meta_done = sem("meta_done")
        top_seq = sem("top_seq")
        oh_done = sem("oh_done")
        msum_done = sem("msum_done")
        acc_seq = sem("acc_seq")
        prod_done = sem("prod_done")
        dest_seq = sem("dest_seq")
        sent = [sem(f"sent{i}") for i in range(2)]
        done_out = sem("done_out")
        bank_ready = [sem(f"bank_ready{i}") for i in range(8)]
        bank_free = [sem(f"bank_free{i}") for i in range(8)]
        tab_pe = sem("tab_pe")
        tab_v = sem("tab_v")
        pads_made = sem("pads_made")
        padded = sem("padded")
        band_made = sem("band_made")
        dummy_out = sem("dummy_out")
        ew_in = sem("expert_weights_in")
        x_in = [sem(f"x_in{i}") for i in range(U)]
        t1_ready, t1_done = sem("t1_ready"), sem("t1_done")
        h_ready, h_done = sem("h_ready"), sem("h_done")
        ktile_done = sem("ktile_done")
        y_ready, y_done = sem("y_ready"), sem("y_done")
        y_sent = [sem(f"y_sent{i}") for i in range(U)]
        yg_in = [sem(f"yg_in{i}") for i in range(2)]
        combined = sem("combined")
        ln2 = sem("ln2")
        ln3 = sem("ln3")
        rstd2 = sem("rstd2")
        rstd3 = sem("rstd3")
        mask_done = sem("mask_done")
        nrow_done = sem("nrow_done")
        expb_done = sem("expb_done")
        rinv_done = sem("rinv_done")
        NTAB = 11
        NCONST = 11
        NCONSTV = 9

        def scatter_chunk(it, k):
            return (it - 2, 0) if k == 7 else (it - 3, k + 1)

        def expert_rounds(eng, step, tail, peeled=1):
            for s in range(U * peeled):
                step(s, s % U, s // U)
            with eng.Fori(peeled, ROUNDS) as rnd:
                for u in range(U):
                    step(rnd * U + u, u, rnd)
            for s in range(tail):
                step(GROUPS + s, s, ROUNDS)

        def column_of(engine, tile):
            return nc.values_load(tile_e[0:1, bass.ds(tile, 1)], (engine,), min_val=0, max_val=C * (NE - 1),
                                  skip_runtime_bounds_check_because="the tile table is clipped to the last expert")

        def row_of(engine, table, n, most):
            return nc.values_load(table[0:1, bass.ds(n, 1)], (engine,), min_val=0, max_val=most,
                                  skip_runtime_bounds_check_because="the tables are within the sorted rows")

        def pad(eng, engine, layer, first):
            eng.wait_ge(pads_made, 2)
            eng.wait_ge(tab_v, NTAB * layer + 2)
            with eng.Fori(0, NE // 16) as e:
                for i in range(8):
                    row = row_of(engine, padrow, e * 8 + (first + i), NE * REGION)
                    eng.dma_start(sorted_d[layer][bass.ds(row, P), :].rearrange("(a b) n -> a (b n)", b=4), pads
                                  ).then_inc(padded, 16)

        block = ctx.enter_context(nc.Block())

        @block.sync
        def _(sp):
            sp.dma_start(x[:, 0:TT, :], x_d.rearrange("(t p) c -> p t c", p=P)[:, 0:TT, :]).then_inc(in_x, 16)
            for dst, src in ((w[:, :], w_d), (bcol[:, :], bcol_d), (trig_col[:, :], trig_col_d),
                             (trig_row[:, :, :].rearrange("p a c -> p (a c)"), trig_row_d.unsqueeze(0).broadcast_to([P, 2 * C]))):
                sp.dma_start(dst, src).then_inc(in_w, 16)
            sp.dma_start(x[:, TT:, :], x_d.rearrange("(t p) c -> p t c", p=P)[:, TT:, :]).then_inc(in_x, 16)
            sp.dma_start(bv[:, :], bv_d.unsqueeze(0).broadcast_to([P, C])).then_inc(in_w, 16)
            sp.dma_start(bproj[:, :], bproj_d.unsqueeze(0).broadcast_to([P, C])).then_inc(in_w, 16)
            for dst, src in ((wproj[:, :], wproj_d), (wb[:, :], wqkv_b_d), (esel[:, :], esel_d)):
                sp.dma_start(dst, src).then_inc(in_w, 16)
            sp.wait_ge(consts_v, NCONSTV)
            for par in range(2):
                for d in (qd, kd):
                    sp.dma_start(d[par, :, 56:64, :], czero).then_inc(rows_init, 16)
                sp.dma_start(qd[par, :, 32:40, :], czero).then_inc(rows_init, 16)
                sp.dma_start(kd[par, :, 35:40, :], czero[0:80, :]).then_inc(rows_init, 16)
                sp.dma_start(kd[par, :, 32:35, :], cone).then_inc(rows_init, 16)

            def write_parts(b):
                par = b % 2
                sp.wait_ge(act_split, 4 * b + 4)
                sp.wait_ge(pool_split, 4 * b + 4)
                if b >= 2:
                    for g in (2 * b - 4, 2 * b - 3):
                        sp.wait_ge(qk_landed[g % 4], 48 * (g // 4 + 1))
                for d, n, groups in ((qd, 0, (parth, parth, parth, partm, None, partm, partl)),
                                     (kd, 1, (partl, partm, parth, parth, None, partm, parth))):
                    for gi, part in enumerate(groups):
                        if part is not None:
                            sp.dma_start(d[par, :, 8 * gi:8 * gi + 8, :], part[:, n, :]).then_inc(parts_out, 16)

            def load_parts(g):
                b, hf, s = g // 2, g % 2, g % 4
                sp.wait_ge(parts_out, 192 * (b + 1))
                sp.wait_ge(rows_init, 160)
                if g >= 4:
                    sp.wait_ge(s2_ready, 20 * (g - 3))
                hs = slice(8 * hf, 8 * hf + 8)
                sp.dma_start(qs[:, s, :, :], qd[b % 2, hs].rearrange("(r h) q n -> (h q) r n", h=2)).then_inc(qk_landed[s], 16)
                for hb in range(2):
                    sp.dma_start(kz[64 * hb:64 * hb + 64, s, hb, :, :],
                                 kd[b % 2, hs].rearrange("(r h) q n -> h q r n", h=2)[hb]).then_inc(qk_landed[s], 16)

            def max_rows(g):
                name = ("MROW1" if g % 2 else "MROW0", g // 2)
                s = g % 4
                sp.wait_ge(misc_free, job[name] + 1)
                sp.dma_start(md[s], mt[:, g % 2, :]).then_inc(mrow_out[g % 2], 16)
                sp.wait_ge(mrow_out[g % 2], 16 * (g // 2 + 1))
                for hb in range(2):
                    sp.dma_start(qs[64 * hb + 32:64 * hb + 36, s, :, :],
                                 md[s].rearrange("(r h q) n -> h q r n", h=2, q=4)[hb]).then_inc(mrow_landed[s], 16)

            for it, k in slots():
                if k == 0 and 0 <= it < B:
                    max_rows(2 * it + 1)
                if k == 3 and 0 <= it + 2 < B:
                    write_parts(it + 2)
                if k == 4:
                    if 0 <= it + 1 < B:
                        max_rows(2 * it + 2)
                    if 0 <= it + 2 < B:
                        load_parts(2 * it + 4)
                if k == 7 and 0 <= it + 2 < B:
                    load_parts(2 * it + 5)

            sp.wait_ge(s2_ready, 5 * B * NP)
            sp.wait_ge(s1_ready, 5 * B * NP)
            sp.wait_ge(pv_done, 4 * B)
            for e in range(0, NE, 16):
                for dst, src in ((kw, keys_d), (vw, values_d)):
                    sp.dma_start(dst[:, C * e:C * (e + 16)].rearrange("p (e n) -> p e n", e=16),
                                 src[e:e + 16].rearrange("e p n -> p e n")).then_inc(ew_in, 16)

            def expert_loads(layer):
                pad(sp, ENG.SP, layer, 0)
                for i in range(2):
                    sp.wait_ge(sent[i], 256 * (B // 2) * (layer + 1))
                sp.wait_ge(padded, 16 * NE * (layer + 1))
                sp.wait_ge(dummy_out, 32)
                sp.wait_ge(tab_v, NTAB * (layer + 1))

                def load(s, u, rnd):
                    if layer or not isinstance(s, int):
                        sp.wait_ge(y_sent[u], (rnd + ROUNDS * layer) * (16 * G))
                    for i in range(G):
                        row = row_of(ENG.SP, tile_r, s * G + i, NE * REGION)
                        sp.dma_start(xin[:, G * u + i, :], sorted_d[layer][bass.ds(row, P), :]).then_inc(x_in[u], 16)

                expert_rounds(sp, load, 0)

            def results(layer, b):
                if b == 0:
                    for u in range(U):
                        sp.wait_ge(y_sent[u], 16 * G * ROUNDS * (layer + 1))
                n = B * layer + b
                if n >= 2:
                    sp.wait_ge(combined, 16 * (n - 1))
                sp.dma_start(yg[:, b % 2, :, :], result_d[layer].rearrange("(n p s) c -> p n (s c)", p=P, s=TOPK)[:, TT * b:TT * b + TT, :]
                             ).then_inc(yg_in[b % 2], 16)

            sp.wait_ge(pads_made, 2)
            for layer in range(2):
                sp.dma_start(sorted_d[layer][NE * REGION:NE * REGION + P, :].rearrange("(a b) n -> a (b n)", b=4), pads).then_inc(dummy_out, 16)
            expert_loads(0)
            for b in range(B):
                results(0, b)
            expert_loads(1)
            for b in range(B):
                results(1, b)
                if b:
                    sp.wait_ge(combined, 16 * (B + b))
                    sp.dma_start(out_d.rearrange("(t p) c -> p t c", p=P)[:, TT * (b - 1):TT * b, :],
                                 x[:, TT * (b - 1):TT * b, :]).then_inc(done_out, 16)
            sp.wait_ge(combined, 16 * 2 * B)
            sp.dma_start(out_d.rearrange("(t p) c -> p t c", p=P)[:, TT * (B - 1):, :], x[:, TT * (B - 1):, :]).then_inc(done_out, 16)
            sp.wait_ge(done_out, 16 * B)

        @block.tensor
        def _(pe):
            def begin(name, b):
                n = job[name, b]
                if n:
                    pe.wait_ge(misc_free, n)

            def scores_kq(pr, u):
                g, p = pr // 4, pr % 4
                s = g % 4
                if p == 0 and u == 0:
                    pe.wait_ge(mrow_landed[s], 32 * (g // 4 + 1))
                v = 5 * pr + u
                if v >= 3:
                    pe.wait_ge(exp_done, v - 2)
                for hb, j, at in KQ_UNITS[u]:
                    n = T - P * j
                    mm = pe.matmul(ps[:, v % 3, at:at + n], kz[:, s, hb, p, P * j:P * j + P],
                                   qs[:, s, p, P * j:T], start=True, stop=True)
                mm.then_inc(s2_ready, 1)

            def scores_qk(pr, u):
                g, p = pr // 4, pr % 4
                s = g % 4
                if p == 0 and u == 0:
                    pe.wait_ge(qk_landed[s], 48 * (g // 4 + 1))
                parts = QK_UNITS[u]
                n = 5 * pr + u
                if n >= 3:
                    pe.wait_ge(s1_free, n - 2)
                for hb, i, at in parts:
                    m = P * (i + 1)
                    pe.matmul(ps[:, 3 + n % 3, at:at + m], qs[:, s, p, P * i:P * i + P], kz[:, s, hb, p, 0:m],
                              start=True, stop=False)
                    mm = pe.matmul(ps[:, 3 + n % 3, at + m - P:at + m], identb[:, :], maskneg[:, :],
                                   start=False, stop=True)
                mm.then_inc(s1_ready, 1)

            def values(grp):
                b = grp // 4
                pe.wait_ge(sel_done, 2 * grp + 2)
                pe.wait_ge(misc_free, job["V", b] + 1)
                if grp:
                    pe.wait_ge(pv_evac, grp)
                for j, width in ((0, 512), (1, 384), (2, 256), (3, 128)):
                    for q in range(4):
                        hb = q % 2
                        at = {0: 1024 * hb, 1: 1024 * hb + 512, 3: 1024 * hb + 896, 2: 2048 + 256 * hb}[j]
                        mm = pe.matmul(ps[32 * q:32 * q + 32, 6, P * j:T],
                                       vaug[:, b % 2, j, 4 * (grp % 4) + q, :],
                                       prob[:, grp % 2, q // 2, at:at + width], start=(j == 0), stop=(j == 3))
                mm.then_inc(pv_done, 1)

            def logits(bank):
                for t in range(TT):
                    mm = pe.matmul(bank[:, NE * t:NE * t + NE], ntt[:, P * t:P * t + P], esel[:, :], start=True, stop=True)
                return mm

            def ranks(bank, layer, b):
                n = B * layer + b
                pe.wait_ge(msum_done, n + 1)
                if n:
                    pe.wait_ge(acc_seq, 2 * n)
                for t in range(TT):
                    o = bank[:, NE * t:NE * t + NE]
                    pe.matmul(o, tri[:, :], msum[:, t, :], start=True, stop=False)
                    for e in range(t):
                        pe.matmul(o, onesb[:, :], msum[:, e, :], start=False, stop=False)
                    mm = pe.matmul(o, onesb[:, :], acc[:, layer, :], start=False, stop=True)
                return mm

            def run(name, b):
                begin(name, b)
                if name[:4] == "MROW":
                    g = 2 * b + (name == "MROW1")
                    pe.wait_ge(mrow_seq, 5 * g + 5)
                    for i in range(TT):
                        mm = pe.transpose(miscb[:, P * i:P * i + P], mparts[:, i, :, :].rearrange("p h s -> p (h s)"), identb[:, :])
                elif name in ("XT", "NT", "YT"):
                    src = {"XT": xn0, "NT": xn1, "YT": ytok}[name]
                    if name != "YT":
                        pe.wait_ge(ln0 if name == "XT" else ln1, 13 * b + 13)
                    for t in range(TT):
                        mm = pe.transpose(misc[:, P * t:P * t + P], src[:, t, :], ident[:, :])
                elif name in ("Q", "K"):
                    pe.wait_ge(rotated, 12)
                    mm = pe.matmul(misc, wqk[:, "QK".index(name), :], xnt[:, b % 2, :], start=True, stop=True)
                elif name == "V":
                    for t in range(TT):
                        mm = pe.matmul(misc[:, P * t:P * t + P], xnt[:, b % 2, P * t:P * t + P], w[:, 4 * C:], start=True, stop=True)
                elif name[0] == "Y":
                    i = int(name[1])
                    for n in range(4):
                        mm = pe.transpose(misc[:, P * n:P * n + P], yts[:, b % 2, n, P * i:P * i + P], ident[:, :])
                elif name == "PJ":
                    for t in range(TT):
                        mm = pe.matmul(misc[:, P * t:P * t + P], yt2[:, P * t:P * t + P], wproj[:, :], start=True, stop=True)
                elif name == "LG":
                    mm = logits(misc)
                elif name == "RK":
                    mm = ranks(misc, 0, b)
                mm.then_inc(misc_ready, 1)

            pe.wait_ge(in_w, 16 * 9)
            pe.wait_ge(consts, NCONST)
            pe.wait_ge(consts_v, NCONSTV)
            for it, k in slots():
                pr = 8 * it + k
                for u in range(5):
                    if 0 <= pr < B * NP:
                        scores_kq(pr, u)
                    if 0 <= pr + NP < B * NP:
                        scores_qk(pr + NP, u)
                    if u == 0 and k % 2 and 0 <= pr - 3 < B * NP:
                        values((pr - 3) // 2)
                    for slot, unit, name, off in JOBS:
                        if (slot, unit) == (k, u) and 0 <= it + off < B:
                            if name == "Y0":
                                pe.wait_ge(pv_evac, 4 * (it + off) + 4)
                            run(name, it + off)

            def tile_table(layer):
                bank = ps[:, 6, :]
                pe.wait_ge(acc_seq, 2 * B * (layer + 1))
                if layer:
                    pe.wait_ge(bank_free[6], bjob["P3", B - 1][1] + 1)
                else:
                    pe.wait_ge(pv_evac, 4 * B)
                v = NTAB * layer
                pe.matmul(bank[0:1, 384:384 + NE], onesb[:, 0:1], acc[:, layer, :], start=True, stop=True)
                pe.matmul(bank[0:NE, 0:1], acc[:, layer, :], onesb[:, 0:1], start=True, stop=True).then_inc(tab_pe, 1)
                pe.wait_ge(tab_v, v + 6)
                pe.matmul(bank[0:NE, 0:1], trii[0:NE, 0:NE], ntile[:, :], start=True, stop=True).then_inc(tab_pe, 1)
                pe.wait_ge(tab_v, v + 8)
                pe.matmul(bank[0:1, 0:NTILES], onesb[0:NE, 0:1], past, start=True, stop=True)
                pe.matmul(bank[0:1, NTILES:2 * NTILES], skip[:, :], past, start=True, stop=True).then_inc(tab_pe, 1)

            def experts(layer):
                pe.wait_ge(tab_v, NTAB * (layer + 1))
                base = GROUPS * layer
                if layer:
                    for i in range(6):
                        pe.wait_ge(bank_free[i], max(n for k, n in bjob.values() if k == i) + 1)
                else:
                    pe.wait_ge(exp_done, 5 * B * NP)
                    pe.wait_ge(s1_free, 5 * B * NP)
                    pe.wait_ge(ew_in, 16 * 8)

                def step(s, u, rnd):
                    static = isinstance(s, int)

                    def late(n):
                        return layer or not static or s >= n

                    def here(n):
                        return not static or 0 <= s - n < GROUPS

                    if here(0):
                        pe.wait_ge(x_in[u], (rnd + ROUNDS * layer + 1) * (16 * G))
                        if late(2):
                            pe.wait_ge(t1_done, s + (base - 1))
                        for i in range(G):
                            mm = pe.transpose(ps[:, u % 2, P * i:P * i + P], xin[:, G * u + i, 0:C], ident[:, :])
                        mm.then_inc(t1_ready, 1)
                    if here(1):
                        v = (u + 1) % 2
                        pe.wait_ge(t1_done, s + base)
                        pe.wait_ge(ktile_done, s + base)
                        if late(3):
                            pe.wait_ge(h_done, s + (base - 2))
                        for i in range(G):
                            mm = pe.matmul(ps[:, 2 + v, P * i:P * i + P], ktile[:, v, P * i:P * i + P], xtt[:, v, P * i:P * i + P],
                                           start=True, stop=True)
                        mm.then_inc(h_ready, 1)
                    if here(2):
                        v = u % 2
                        pe.wait_ge(h_done, s + (base - 1))
                        if late(4):
                            pe.wait_ge(y_done, s + (base - 3))
                        for i in range(G):
                            col = column_of(ENG.PE, (s - 2) * G + i)
                            mm = pe.matmul(ps[:, 4 + v, P * i:P * i + P], hidt[:, v, P * i:P * i + P], vw[:, bass.ds(col, C)],
                                           start=True, stop=True)
                        mm.then_inc(y_ready, 1)

                expert_rounds(pe, step, 2)

            def attention_b(name, b):
                bank, n = bjob[name, b]
                o = ps[:, bank, :]
                if n:
                    pe.wait_ge(bank_free[bank], n)
                elif bank < 6:
                    pe.wait_ge((t1_done, h_done, y_done)[bank // 2], GROUPS)
                elif bank == 6:
                    pe.wait_ge(tab_v, NTAB)
                else:
                    pe.wait_ge(misc_free, len(job))
                i = int(name[1]) if name[0] in "SPO" else 0
                if name == "XT":
                    pe.wait_ge(ln2, 13 * b + 13)
                    for t in range(TT):
                        mm = pe.transpose(o[:, P * t:P * t + P], xn0[:, t, :], ident[:, :])
                elif name == "NT":
                    pe.wait_ge(ln3, 13 * b + 13)
                    for t in range(TT):
                        mm = pe.transpose(o[:, P * t:P * t + P], xn1[:, t, :], ident[:, :])
                elif name in ("Q", "K"):
                    pe.wait_ge(bank_free[0], bjob["XT", b][1] + 1)
                    c = C * "QK".index(name)
                    mm = pe.matmul(o, wb[:, c:c + C], xnt[:, b % 2, :], start=True, stop=True)
                elif name == "V":
                    for t in range(TT):
                        mm = pe.matmul(o[:, P * t:P * t + P], xnt[:, b % 2, P * t:P * t + P], wb[:, 2 * C:], start=True, stop=True)
                elif name == "LG":
                    pe.wait_ge(bank_free[0], bjob["NT", b][1] + 1)
                    mm = logits(o)
                elif name == "RK":
                    mm = ranks(o, 1, b)
                elif name[0] == "S":
                    pe.wait_ge(bank_free[1], bjob["Q", b][1] + 1)
                    pe.wait_ge(bank_free[2], bjob["K", b][1] + 1)
                    mm = pe.matmul(o, qkv[b % 2][0][:, P * i:P * i + P], qkv[b % 2][1], start=True, stop=True)
                elif name[0] == "P":
                    pe.wait_ge(expb_done, TT * b + i + 1)
                    for j in range(TT):
                        mm = pe.transpose(o[:, P * j:P * j + P], probb[:, i % 2, P * j:P * j + P], ident[:, :])
                elif name[0] == "O":
                    pe.wait_ge(bank_free[6], bjob[f"P{i}", b][1] + 1)
                    pe.wait_ge(bank_free[3], bjob["V", b][1] + 1)
                    for j in range(TT):
                        mm = pe.matmul(o[:, 0:C], probt[:, i % 2, P * j:P * j + P], qkv[b % 2][2][:, P * j:P * j + P],
                                       start=(j == 0), stop=(j == TT - 1))
                mm.then_inc(bank_ready[bank], 1)

            tile_table(0)
            experts(0)
            for it in range(-1, LAST_IT_B + 1):
                for _, name, off in BJOBS:
                    if 0 <= it + off < B:
                        attention_b(name, it + off)
            tile_table(1)
            experts(1)

        @block.scalar
        def _(act):
            def take(name, b):
                act.wait_ge(misc_ready, job[name, b] + 1)

            for it, k in slots():
                pr = 8 * it + k
                for u in range(5):
                    if 0 <= pr < B * NP:
                        grp, v = pr // 2, 5 * pr + u
                        if pr % 2 == 0 and u == 0 and grp >= 2:
                            act.wait_ge(pv_done, grp - 1)
                        act.wait_ge(s2_ready, v + 1)
                        nc.scalar.activation(prob[:, grp % 2, pr % 2, T * u:T * u + T], ps[:, v % 3, :], ACT.Exp,
                                             scale=SCALE_A).then_inc(exp_done, 1)
                    if u == 3 and k % 2 and 0 <= pr - 3 < B * NP:
                        grp = (pr - 3) // 2
                        b = grp // 4
                        act.wait_ge(pv_done, grp + 1)
                        if b >= 2:
                            act.wait_ge(misc_ready, job["Y3", b - 2] + 1)
                        nc.scalar.copy(yts[:, b % 2, grp % 4, :], pv).then_inc(pv_evac, 1)
                    if (k, u) == (0, 1) and 0 <= it < B:
                        g = 2 * it + 1
                        take("MROW1", it)
                        if g >= 2:
                            act.wait_ge(mrow_out[1], 16 * (g // 2))
                        nc.scalar.copy(mt[:, 1, :], miscb[:, 0:T]).then_inc(misc_free, 1)
                    if (k, u) == (0, 2) and 0 <= it + 2 < B:
                        take("XT", it + 2)
                        nc.scalar.copy(xnt[:, it % 2, :], misc).then_inc(misc_free, 1)
                    if (k, u) == (1, 1) and 0 <= it - 2 < B:
                        take("NT", it - 2)
                        nc.scalar.copy(ntt[:, :], misc).then_inc(misc_free, 1)
                    if (k, u) == (1, 4) and 0 <= it - 2 < B:
                        b = it - 2
                        if b >= 2:
                            act.wait_ge(sent[b % 2], 256 * (b // 2))
                        for t in range(TT):
                            nc.scalar.copy(xs[:, b % 2, t, :, 0:C],
                                           xn1[:, t, :].unsqueeze(1).broadcast_to([P, TOPK, C])).then_inc(xs_filled, 1)
                    if (k, u) == (2, 2) and 0 <= it - 2 < B:
                        b = it - 2
                        take("LG", b)
                        if b:
                            act.wait_ge(top_seq, 11 * (b - 1) + 10)
                        nc.scalar.activation(sg[:, :, :].rearrange("p t e -> p (t e)"), misc[:, 0:TT * NE], ACT.Exp,
                                             scale=-1.0).then_inc(misc_free, 1)
                    if (k, u) == (2, 3) and 0 <= it + 2 < B:
                        b = it + 2
                        act.wait_ge(misc_free, job["K", b] + 1)
                        act.wait_ge(rows_init, 160)
                        if b:
                            act.wait_ge(parts_out, 192 * b)
                        for n in range(2):
                            nc.scalar.copy(parth[:, n, :], ropea[:, n, :]).then_inc(act_split, 1)
                    if (k, u) == (3, 2) and 0 <= it + 2 < B:
                        b = it + 2
                        for n in range(2):
                            act.wait_ge(pool_split, 4 * b + 1 + n)
                            nc.scalar.copy(partm[:, n, :], ropeb[:, n, :]).then_inc(act_split, 1)
                    if (k, u) == (4, 1) and 0 <= it + 1 < B:
                        g = 2 * it + 2
                        take("MROW0", it + 1)
                        if g >= 2:
                            act.wait_ge(mrow_out[0], 16 * (g // 2))
                        nc.scalar.copy(mt[:, 0, :], miscb[:, 0:T]).then_inc(misc_free, 1)
                    if (k, u) == (6, 2) and 0 <= it - 1 < B:
                        take("YT", it - 1)
                        nc.scalar.copy(yt2[:, :], misc).then_inc(misc_free, 1)

            def experts(layer):
                base = GROUPS * layer
                pad(act, ENG.Activation, layer, NE // 2)
                if layer:
                    act.wait_ge(bank_ready[7], bjob["O3", B - 1][1] + 1)
                else:
                    act.wait_ge(misc_ready, job["Y3", B - 1] + 1)
                    act.wait_ge(ew_in, 16 * 8)
                act.wait_ge(tab_v, NTAB * (layer + 1))

                def step(s, u, rnd):
                    if layer or not isinstance(s, int) or s >= 2:
                        act.wait_ge(h_ready, s + (base - 1))
                    for i in range(G):
                        col = column_of(ENG.Activation, s * G + i)
                        cp = nc.scalar.copy(ktile[:, u % 2, P * i:P * i + P], kw[:, bass.ds(col, C)])
                    cp.then_inc(ktile_done, 1)

                expert_rounds(act, step, 0)

            def bank_take(name, b):
                bank, n = bjob[name, b]
                act.wait_ge(bank_ready[bank], n + 1)
                return ps[:, bank, :], bank_free[bank]

            def attention_b(name, b):
                o, free = bank_take(name, b) if name[0] != "E" else (None, None)
                i = int(name[1]) if name[0] in "EP" else 0
                if name == "XT":
                    if b >= 2:
                        act.wait_ge(bank_ready[3], b - 1)
                    nc.scalar.copy(xnt[:, b % 2, :], o).then_inc(free, 1)
                elif name == "NT":
                    nc.scalar.copy(ntt[:, :], o).then_inc(free, 1)
                    n = B + b
                    act.wait_ge(sent[b % 2], 256 * (n // 2))
                    for t in range(TT):
                        nc.scalar.copy(xs[:, b % 2, t, :, 0:C],
                                       xn1[:, t, :].unsqueeze(1).broadcast_to([P, TOPK, C])).then_inc(xs_filled, 1)
                elif name == "Q":
                    if b >= 2:
                        act.wait_ge(bank_ready[5], bjob["S3", b - 2][1] + 1)
                    nc.scalar.copy(qkv[b % 2][0], o).then_inc(free, 1)
                elif name == "V":
                    if b >= 2:
                        act.wait_ge(bank_ready[7], bjob["O3", b - 2][1] + 1)
                    nc.scalar.copy(qkv[b % 2][2], o).then_inc(free, 1)
                elif name == "LG":
                    act.wait_ge(top_seq, 11 * (B + b - 1) + 10)
                    nc.scalar.activation(sg[:, :, :].rearrange("p t e -> p (t e)"), o[:, 0:TT * NE], ACT.Exp,
                                         scale=-1.0).then_inc(free, 1)
                elif name[0] == "E":
                    n = TT * b + i
                    act.wait_ge(nrow_done, n + 1)
                    if n >= 2:
                        bank, k = bjob[f"P{(n - 2) % TT}", (n - 2) // TT]
                        act.wait_ge(bank_ready[bank], k + 1)
                    if n >= TT:
                        act.wait_ge(rinv_done, n - TT + 1)
                    nc.scalar.activation(probb[:, i % 2, :], masked[:, i % 2, :], ACT.Exp, bias=nrow[:, i:i + 1],
                                         scale=SCALE_B, accum_out=rowsum[:, i:i + 1]).then_inc(expb_done, 1)
                elif name[0] == "P":
                    n = TT * b + i
                    if n >= 2:
                        bank, k = bjob[f"O{(n - 2) % TT}", (n - 2) // TT]
                        act.wait_ge(bank_ready[bank], k + 1)
                    nc.scalar.copy(probt[:, i % 2, :], o).then_inc(free, 1)

            experts(0)
            for it in range(-1, LAST_IT_B + 1):
                for name, off in (("E0", 0), ("E1", 0), ("NT", -1), ("P0", 0), ("E2", 0), ("XT", 1), ("P1", 0), ("E3", 0),
                                  ("LG", -1), ("Q", 1), ("P2", 0), ("V", 1), ("P3", 0)):
                    if 0 <= it + off < B:
                        attention_b(name, it + off)
            experts(1)

        @block.vector
        def _(dve):
            def take(name, b):
                dve.wait_ge(misc_ready, job[name, b] + 1)

            def ln_stats(src, st, mv, rs, b, seq):
                for t in range(TT):
                    nc.vector.bn_stats(st[:, t, :], src[:, t, :]).then_inc(seq, 1)
                dve.wait_ge(seq, 13 * b + 4)
                for t in range(TT):
                    nc.vector.bn_aggr(mv[:, t, :], st[:, t, :]).then_inc(seq, 1)
                dve.wait_ge(seq, 13 * b + 8)
                nc.vector.tensor_scalar(rs[:, :], mv[:, :, 1], EPS, None, ALU.add).then_inc(seq, 1)

            def ln_apply(src, mv, rs, dst, b, seq, rstd):
                dve.wait_ge(rstd, b + 1)
                for t in range(TT):
                    nc.vector.tensor_scalar(dst[:, t, :], src[:, t, :], mv[:, t, 0:1], rs[:, t:t + 1],
                                            ALU.subtract, ALU.mult).then_inc(seq, 1)

            def maxima(pr, u):
                p = pr % 4
                if p == 0 and u == 0 and pr:
                    dve.wait_ge(mrow_seq, 5 * (pr // 4 - 1) + 1)
                n = 5 * pr + u
                dve.wait_ge(s1_ready, n + 1)
                if u == 4:
                    nc.vector.tensor_reduce(mx[:, 1, 2 * p:2 * p + 2], ps[:, 3 + n % 3, :].rearrange("p (h n) -> p h n", h=2),
                                            AX.X, ALU.max).then_inc(s1_free, 1)
                    return
                for hb, i, at in QK_UNITS[u]:
                    red = nc.vector.tensor_reduce(mx[:, i, 2 * p + hb:2 * p + hb + 1],
                                                  ps[:, 3 + n % 3, at:at + P * (i + 1)], AX.X, ALU.max)
                red.then_inc(s1_free, 1)

            def max_parts(g):
                dve.wait_ge(s1_free, 20 * g + 20)
                nc.vector.tensor_scalar(mneg[:, :, :], mx[:, :, :], -1.0, None, ALU.mult).then_inc(mrow_seq, 1)
                dve.wait_ge(mrow_seq, 5 * g + 1)
                if g:
                    dve.wait_ge(misc_ready, job["MROW0" if g % 2 else "MROW1", (g - 1) // 2] + 1)
                nc.vector.tensor_copy(mparts[:, :, :, 0], mneg[:, :, :]).then_inc(mrow_seq, 1)
                dve.wait_ge(mrow_seq, 5 * g + 2)
                nc.vector.tensor_tensor(mres[:, :, :], mneg[:, :, :], mparts[:, :, :, 0], ALU.subtract).then_inc(mrow_seq, 1)
                dve.wait_ge(mrow_seq, 5 * g + 3)
                nc.vector.tensor_copy(mparts[:, :, :, 1], mres[:, :, :]).then_inc(mrow_seq, 1)
                dve.wait_ge(mrow_seq, 5 * g + 4)
                nc.vector.tensor_tensor(mparts[:, :, :, 2], mres[:, :, :], mparts[:, :, :, 1], ALU.subtract).then_inc(mrow_seq, 1)

            def rotate_weights():
                for n in range(2):
                    at = 6 * n
                    for m in range(2):
                        nc.vector.tensor_tensor(wrot[:, m, :], w[:, C * (2 * n + m):C * (2 * n + m + 1)], trig_row[:, m, :],
                                                ALU.mult).then_inc(rotated, 1)
                    dve.wait_ge(rotated, at + 2)
                    nc.vector.tensor_tensor(wqk[:, n, :], wrot[:, 0, :], wrot[:, 1, :], ALU.add).then_inc(rotated, 1)
                    for m in range(2):
                        nc.vector.tensor_tensor(brot[:, m:m + 1], bcol[:, 2 * n + m:2 * n + m + 1], trig_col[:, m:m + 1],
                                                ALU.mult).then_inc(rotated, 1)
                    dve.wait_ge(rotated, at + 5)
                    nc.vector.tensor_tensor(bqk[:, n:n + 1], brot[:, 0:1], brot[:, 1:2], ALU.add).then_inc(rotated, 1)
                    dve.wait_ge(rotated, at + 6)

            def add_bias(name, b):
                n = "QK".index(name)
                take(name, b)
                if b:
                    dve.wait_ge(pool_split, 4 * b)
                nc.vector.tensor_scalar(ropea[:, n, :], misc, bqk[:, n:n + 1], None, ALU.add).then_inc(misc_free, 1)

            def head_outputs(i, b):
                take(f"Y{i}", b)
                m = misc.rearrange("p (h d) -> p h d", h=NH)
                if i or b:
                    dve.wait_ge(misc_free, job[f"Y{i}", b])
                nc.vector.reciprocal(yrc[:, :], m[:, :, HD]).then_inc(yrc_done, 1)
                dve.wait_ge(yrc_done, 4 * b + i + 1)
                nc.vector.tensor_tensor(ytok[:, i, :].rearrange("p (h d) -> p h d", h=NH), m[:, :, 0:HD],
                                        yrc[:, :].unsqueeze(2).broadcast_to([P, NH, HD]), ALU.mult).then_inc(misc_free, 1)

            def choose(b, exp_done_sem, exp_done_n):
                dve.wait_ge(exp_done_sem, exp_done_n)
                if b:
                    dve.wait_ge(top_seq, 11 * b)
                nc.vector.tensor_scalar(sg[:, :, :], sg[:, :, :], 1.0, None, ALU.add).then_inc(top_seq, 1)
                dve.wait_ge(top_seq, 11 * b + 1)
                nc.vector.reciprocal(sg[:, :, :], sg[:, :, :]).then_inc(top_seq, 1)
                dve.wait_ge(top_seq, 11 * b + 2)
                for t in range(TT):
                    nc.vector.max(top[:, TT * (b % B) + t, :], sg[:, t, :]).then_inc(top_seq, 1)
                for t in range(TT):
                    dve.wait_ge(top_seq, 11 * b + 3 + t)
                    nc.vector.max_index(idx8[:, t, :], top[:, TT * (b % B) + t, :], sg[:, t, :]).then_inc(top_seq, 1)
                dve.wait_ge(top_seq, 11 * b + 10)
                nc.vector.tensor_copy(idxf[:, :, :], idx8[:, :, 0:TOPK]).then_inc(top_seq, 1)
                dve.wait_ge(top_seq, 11 * b + 11)
                if b:
                    dve.wait_ge(prod_done, b)
                nc.vector.tensor_tensor(oh[:, :, :, :].rearrange("p t s e -> p (t s) e"),
                                        iota_e[:, :].unsqueeze(1).broadcast_to([P, TT * TOPK, NE]),
                                        idxf[:, :, :].rearrange("p t s -> p (t s)").unsqueeze(2).broadcast_to([P, TT * TOPK, NE]),
                                        ALU.is_equal).then_inc(oh_done, 1)

            def chosen(b, rank_sem, rank_n):
                dve.wait_ge(oh_done, b + 1)
                if b:
                    dve.wait_ge(rank_sem, rank_n)
                with nc.allow_low_precision(reason="0 and 1 are exact"):
                    nc.vector.tensor_reduce(msum[:, :, :], oh[:, :, :, :].rearrange("p t s e -> p t e s"), AX.X,
                                            ALU.add).then_inc(msum_done, 1)

            def positions(b, bank, free):
                layer = b // B
                if b:
                    dve.wait_ge(prod_done, b)
                nc.vector.tensor_tensor(rpos[:, :, :], bank[:, 0:TT * NE].rearrange("p (t e) -> p t e", t=TT),
                                        ebase[:, :].unsqueeze(1).broadcast_to([P, TT, NE]), ALU.add).then_inc(free, 1)
                with nc.allow_low_precision(reason="counts up to 32 are exact"):
                    nc.vector.tensor_reduce(tsum[:, :], msum[:, :, :].rearrange("p t e -> p e t"), AX.X,
                                            ALU.add).then_inc(acc_seq, 1)
                dve.wait_ge(acc_seq, 2 * b + 1)
                nc.vector.tensor_tensor(acc[:, layer, :], acc[:, layer, :], tsum[:, :], ALU.add).then_inc(acc_seq, 1)

            def destinations(b):
                dve.wait_ge(prod_done, b + 1)
                if b:
                    dve.wait_ge(dest_seq, 2 * b)
                nc.vector.tensor_reduce(destf[:, :], prod[:, :, :, :].rearrange("p t s e -> p (t s) e"), AX.X,
                                        ALU.add).then_inc(dest_seq, 1)
                dve.wait_ge(dest_seq, 2 * b + 1)
                nc.vector.tensor_copy(dest[:, 16 * (b % B):16 * (b % B) + 16], destf[:, :]).then_inc(dest_seq, 1)

            nc.vector.memset(czero, 0.0).then_inc(consts_v, 1)
            nc.vector.memset(cone, 1.0).then_inc(consts_v, 1)
            nc.vector.memset(mhalf[:, :], -0.5).then_inc(consts_v, 1)
            nc.vector.memset(acc[:, :, :], 0.0).then_inc(consts_v, 1)
            nc.vector.memset(mparts[:, :, :, 3], 0.0).then_inc(consts_v, 1)
            nc.vector.memset(kz[64:128, :, 0, :, :], 0.0).then_inc(consts_v, 1)
            nc.vector.memset(kz[0:64, :, 1, :, :], 0.0).then_inc(consts_v, 1)
            nc.vector.memset(vaug[:, :, :, :, HD + 1:32], 0.0).then_inc(consts_v, 1)
            nc.vector.memset(vaug[:, :, :, :, HD:HD + 1], 1.0).then_inc(consts_v, 1)
            dve.wait_ge(in_w, 16 * 9)
            dve.wait_ge(in_x, 32)
            dve.wait_ge(consts, NCONST)
            rotate_weights()
            for it, k in slots():
                pr = 8 * it + k + NP
                pre, post, last, nxt = it + 2, it - 1, it - 2, it + 3
                for u in range(5):
                    if 0 <= pr < B * NP:
                        maxima(pr, u)
                        if pr % 4 == 3 and u == 4:
                            max_parts(pr // 4)
                    at = (k, u)
                    if at == (0, 2) and 0 <= last < B:
                        if last:
                            dve.wait_ge(xs_filled, TT * last)
                        ln_apply(x[:, TT * last:TT * last + TT, :], mv1, rs1, xn1, last, ln1, rstd1)
                    if at == (1, 2) and 0 <= pre < B:
                        add_bias("Q", pre)
                    if at == (1, 3) and 0 <= pre < B:
                        add_bias("K", pre)
                    if at == (2, 4) and 0 <= last < B:
                        choose(last, misc_free, job["LG", last] + 1)
                    if at == (3, 0) and 0 <= last < B:
                        chosen(last, misc_ready, job["RK", last - 1] + 1 if last else 0)
                    if at == (3, 1) and 0 <= it + 1 < B:
                        b = it + 1
                        take("V", b)
                        if b >= 2:
                            dve.wait_ge(pv_done, 4 * (b - 2) + 4)
                        nc.vector.tensor_tensor(
                            vaug[:, b % 2, :, :, 0:HD], misc.rearrange("p (t h d) -> p t h d", t=TT, h=NH),
                            bv[:, :].rearrange("p (h d) -> p h d", h=NH).unsqueeze(1).broadcast_to([P, TT, NH, HD]),
                            ALU.add).then_inc(misc_free, 1)
                    if at in ((3, 3), (4, 3), (5, 1), (5, 3)) and 0 <= post < B:
                        head_outputs({(3, 3): 0, (4, 3): 1, (5, 1): 2, (5, 3): 3}[at], post)
                    if at == (4, 2) and 0 <= last < B:
                        take("RK", last)
                        positions(last, misc, misc_free)
                    if at == (4, 4) and 0 <= nxt < B:
                        ln_stats(x[:, TT * nxt:TT * nxt + TT, :], st0, mv0, rs0, nxt, ln0)
                    if at == (6, 3) and 0 <= nxt < B:
                        if nxt:
                            dve.wait_ge(misc_ready, job["XT", nxt - 1] + 1)
                        ln_apply(x[:, TT * nxt:TT * nxt + TT, :], mv0, rs0, xn0, nxt, ln0, rstd0)
                    if at == (6, 4) and 0 <= last < B:
                        destinations(last)
                    if at == (7, 2) and 0 <= post < B:
                        b = post
                        take("PJ", b)
                        dve.wait_ge(xb_done, b + 1)
                        nc.vector.tensor_tensor(x[:, TT * b:TT * b + TT, :], misc.rearrange("p (t c) -> p t c", t=TT),
                                                x[:, TT * b:TT * b + TT, :], ALU.add).then_inc(misc_free, 1)
                        dve.wait_ge(misc_free, job["PJ", b] + 1)
                        ln_stats(x[:, TT * b:TT * b + TT, :], st1, mv1, rs1, b, ln1)

            def tile_table(layer):
                bank = ps[:, 6, :]
                v, q = NTAB * layer, 3 * layer
                dve.wait_ge(tab_pe, q + 1)
                nc.vector.tensor_copy(count[:, :], bank[0:NE, 0:1]).then_inc(tab_v, 1)
                dve.wait_ge(tab_v, v + 1)
                nc.vector.tensor_tensor(padrow[:, :], bank[0:1, 384:384 + NE], ebase[0:1, :], ALU.add).then_inc(tab_v, 1)
                nc.vector.tensor_scalar(ceil_i[:, :], count[:, :], float(P - 1), None, ALU.add).then_inc(tab_v, 1)
                dve.wait_ge(tab_v, v + 3)
                nc.vector.tensor_scalar(ceil_s[:, :], ceil_i[:, :], 7, None, ALU.arith_shift_right).then_inc(tab_v, 1)
                dve.wait_ge(tab_v, v + 4)
                nc.vector.tensor_copy(ntile[:, :], ceil_s[:, :]).then_inc(tab_v, 1)
                dve.wait_ge(tab_v, v + 5)
                nc.vector.tensor_scalar(skip[:, :], ntile[:, :], -1.0, float(REGION // P), ALU.mult, ALU.add).then_inc(tab_v, 1)
                dve.wait_ge(tab_pe, q + 2)
                nc.vector.tensor_copy(upto[:, :], bank[0:NE, 0:1]).then_inc(tab_v, 1)
                dve.wait_ge(tab_v, v + 7)
                nc.vector.tensor_scalar(past, iota_t[:, :], upto[:, 0:1], None, ALU.is_ge).then_inc(tab_v, 1)
                dve.wait_ge(tab_pe, q + 3)
                nc.vector.tensor_scalar(tile_e, bank[0:1, 0:NTILES], float(NE - 1), float(C), ALU.min,
                                        ALU.mult).then_inc(tab_v, 1)
                nc.vector.tensor_tensor(rowf, bank[0:1, NTILES:2 * NTILES], iota_t[0:1, :], ALU.add).then_inc(tab_v, 1)
                dve.wait_ge(tab_v, v + 10)
                nc.vector.tensor_scalar(tile_r, rowf, float(DUMMY), float(P), ALU.min, ALU.mult).then_inc(tab_v, 1)

            def experts(layer):
                base = GROUPS * layer
                if layer:
                    dve.wait_ge(bank_ready[7], bjob["O3", B - 1][1] + 1)
                    dve.wait_ge(combined, 16 * B)
                else:
                    dve.wait_ge(misc_ready, job["Y3", B - 1] + 1)
                    dve.wait_ge(pv_done, 4 * B)

                def step(s, u, rnd):
                    static = isinstance(s, int)
                    if not static or s < GROUPS:
                        dve.wait_ge(t1_ready, s + (base + 1))
                        if layer or not static or s >= 2:
                            dve.wait_ge(h_ready, s + (base - 1))
                        nc.vector.tensor_copy(xtt[:, u % 2, :], ps[:, u % 2, :]).then_inc(t1_done, 1)
                    if not static or 1 <= s < GROUPS + 1:
                        v = (u + 1) % 2
                        dve.wait_ge(h_ready, s + base)
                        if layer or not static or s >= 3:
                            dve.wait_ge(y_ready, s + (base - 2))
                        nc.vector.tensor_scalar(hidt[:, v, :], ps[:, 2 + v, :], 0.0, None, ALU.max).then_inc(h_done, 1)
                    if not static or s >= 2:
                        v, q = u % 2, (u - 2) % U
                        dve.wait_ge(y_ready, s + (base - 1))
                        done = rnd + (ROUNDS * layer if u >= 2 else ROUNDS * layer - 1)
                        if not isinstance(done, int) or done > 0:
                            dve.wait_ge(y_sent[q], done * (16 * G))
                        nc.vector.tensor_copy(yout[:, G * q:G * q + G, :],
                                              ps[:, 4 + v, :].rearrange("p (g n) -> p g n", g=G)).then_inc(y_done, 1)

                expert_rounds(dve, step, 2, 2)

            def combine(layer, b):
                n = B * layer + b
                dve.wait_ge(yg_in[b % 2], 16 * (n // 2 + 1))
                for c in range(TOPK):
                    dve.wait_ge(combined, 16 * n + TT * c)
                    for t in range(TT):
                        xt = x[:, TT * b + t, :]
                        nc.vector.scalar_tensor_tensor(out=xt, in0=yg[:, b % 2, t, C * c:C * c + C],
                                                       scalar=top[:, TT * b + t, c:c + 1], in1=xt,
                                                       op0=ALU.mult, op1=ALU.add).then_inc(combined, 1)

            def bank_take(name, b):
                bank, n = bjob[name, b]
                dve.wait_ge(bank_ready[bank], n + 1)
                return ps[:, bank, :], bank_free[bank]

            def score_rows(i, b):
                n = TT * b + i
                o, free = bank_take(f"S{i}", b)
                if n >= 2:
                    dve.wait_ge(expb_done, n - 1)
                nc.vector.tensor_tensor_reduce(out=masked[:, i % 2, :], in0=o, in1=band[:, i, :], scale=1.0,
                                               scalar=-3.0e38, op0=ALU.mult, op1=ALU.max,
                                               accum_out=rowmax[:, i:i + 1]).then_inc(free, 1)
                bank, k = bjob[f"S{i}", b]
                dve.wait_ge(bank_free[bank], k + 1)
                nc.vector.tensor_scalar(nrow[:, i:i + 1], rowmax[:, i:i + 1], -SCALE_B, None, ALU.mult).then_inc(nrow_done, 1)

            def score_out(i, b):
                n = TT * b + i
                dve.wait_ge(expb_done, n + 1)
                nc.vector.reciprocal(rinv[:, i:i + 1], rowsum[:, i:i + 1]).then_inc(rinv_done, 1)
                dve.wait_ge(rinv_done, n + 1)
                o, free = bank_take(f"O{i}", b)
                xt = x[:, TT * b + i, :]
                nc.vector.scalar_tensor_tensor(out=xt, in0=o[:, 0:C], scalar=rinv[:, i:i + 1], in1=xt,
                                               op0=ALU.mult, op1=ALU.add).then_inc(free, 1)

            def combine_and_stats(b):
                combine(0, b)
                dve.wait_ge(combined, 16 * b + 16)
                ln_stats(x[:, TT * b:TT * b + TT, :], st0, mv0, rs0, b, ln2)

            tile_table(0)
            experts(0)
            dve.wait_ge(band_made, 3)
            for b in range(-1, LAST_IT_B + 1):
                r, nxt = b - 1, b + 1
                attend, route, prepare = 0 <= b < B, 0 <= r < B, nxt < B
                if attend:
                    score_rows(0, b)
                    score_rows(1, b)
                if route:
                    dve.wait_ge(xs_filled, TT * (B + r))
                    ln_apply(x[:, TT * r:TT * r + TT, :], mv1, rs1, xn1, r, ln3, rstd3)
                if prepare:
                    combine_and_stats(nxt)
                if attend:
                    score_out(0, b)
                    score_rows(2, b)
                if prepare:
                    if nxt:
                        dve.wait_ge(bank_ready[0], bjob["XT", b][1] + 1)
                    ln_apply(x[:, TT * nxt:TT * nxt + TT, :], mv0, rs0, xn0, nxt, ln2, rstd2)
                if attend:
                    score_out(1, b)
                    score_rows(3, b)
                if route:
                    bank, n = bjob["LG", r]
                    choose(B + r, bank_free[bank], n + 1)
                    if r:
                        bank, n = bjob["RK", r - 1]
                        chosen(B + r, bank_ready[bank], n + 1)
                    else:
                        chosen(B, misc_ready, len(job))
                if prepare:
                    o, free = bank_take("K", nxt)
                    if nxt >= 2:
                        dve.wait_ge(bank_ready[5], bjob["S3", nxt - 2][1] + 1)
                    nc.vector.tensor_copy(qkv[nxt % 2][1], o).then_inc(free, 1)
                if attend:
                    score_out(2, b)
                if route:
                    o, free = bank_take("RK", r)
                    positions(B + r, o, free)
                if attend:
                    score_out(3, b)
                    dve.wait_ge(bank_free[7], bjob["O3", b][1] + 1)
                    if b:
                        dve.wait_ge(ln3, 13 * b)
                    ln_stats(x[:, TT * b:TT * b + TT, :], st1, mv1, rs1, b, ln3)
                if route:
                    if r == 0:
                        for i in range(2):
                            dve.wait_ge(sent[i], 256 * (B // 2))
                    destinations(B + r)
            tile_table(1)
            experts(1)
            for b in range(B):
                combine(1, b)

        @block.gpsimd
        def _(pool):
            g = nc.gpsimd
            g.memset(ident[:, :], 0.0).then_inc(consts, 1)
            g.memset(maskneg[:, :], 0.0).then_inc(consts, 1)
            g.memset(onesb[:, :], 1.0).then_inc(consts, 1)
            g.memset(xs[:, :, :, :, C + 1:ROW], 0.0).then_inc(consts, 1)
            g.iota(iota_e[:, :], pattern=[[1, NE]], base=0, channel_multiplier=0,
                   allow_small_or_imprecise_dtypes=True).then_inc(consts, 1)
            g.iota(ebase[:, :], pattern=[[REGION, NE]], base=0, channel_multiplier=0,
                   allow_small_or_imprecise_dtypes=True).then_inc(consts, 1)
            pool.wait_ge(consts, 6)
            g.affine_select(out=ident[:, :], in_=ident[:, :], compare_op=ALU.not_equal, fill=1.0, base=0,
                            pattern=[[-1, P]], channel_multiplier=1).then_inc(consts, 1)
            g.affine_select(out=maskneg[:, :], in_=maskneg[:, :], compare_op=ALU.is_ge, fill=NEG, base=0,
                            pattern=[[-1, P]], channel_multiplier=1)
            g.affine_select(out=tri[:, :], in_=onesb[:, :], compare_op=ALU.is_gt, fill=0.0, base=0,
                            pattern=[[1, P]], channel_multiplier=-1).then_inc(consts, 1)
            g.affine_select(out=trii[:, :], in_=onesb[:, :], compare_op=ALU.is_ge, fill=0.0, base=0,
                            pattern=[[1, P]], channel_multiplier=-1).then_inc(consts, 1)
            g.iota(iota_t[:, :], pattern=[[1, NTILES]], base=0, channel_multiplier=0,
                   allow_small_or_imprecise_dtypes=True).then_inc(consts, 1)
            pool.wait_ge(consts, 7)
            g.tensor_copy(identb[:, :], ident[:, :]).then_inc(consts, 1)

            pool.wait_ge(in_w, 16 * 9)
            pool.wait_ge(consts_v, NCONSTV)
            for it, k in slots():
                if k == 0 and 0 <= it - 2 < B:
                    pool.wait_ge(ln1, 13 * (it - 2) + 9)
                    g.tensor_tensor(rs1[:, :], rs1[:, :], mhalf[:, :], ALU.pow).then_inc(rstd1, 1)
                if k == 5 and 0 <= it + 3 < B:
                    pool.wait_ge(ln0, 13 * (it + 3) + 9)
                    g.tensor_tensor(rs0[:, :], rs0[:, :], mhalf[:, :], ALU.pow).then_inc(rstd0, 1)
                pr = 8 * it + k
                if 0 <= pr < B * NP:
                    pool.wait_ge(exp_done, 5 * pr + 5)
                    pb = prob[:, (pr // 2) % 2, pr % 2, :]
                    for lo, hi, n in ((0, 2048, 4), (2048, 2560, 2)):
                        v = pb[:, lo:hi].rearrange("p (a n) -> p a n", a=n)[:, :, 0:P]
                        g.affine_select(out=v, in_=v, compare_op=ALU.is_ge, fill=0.0, base=0,
                                        pattern=[[0, n], [1, P]], channel_multiplier=-1)
                    v = pb[:, 0:2048].rearrange("p (a n) -> p a n", a=2)[:, :, 896:1024]
                    g.affine_select(out=v, in_=v, compare_op=ALU.is_ge, fill=0.0, base=0,
                                    pattern=[[0, 2], [1, P]], channel_multiplier=-1).then_inc(sel_done, 1)
                b = it + 2
                if 0 <= b < B:
                    if k == 0:
                        pool.wait_ge(ln0, 13 * b + 13)
                        xb = x[:, TT * b:TT * b + TT, :]
                        g.tensor_tensor(xb, xb, bproj[:, :].unsqueeze(1).broadcast_to([P, TT, C]), ALU.add).then_inc(xb_done, 1)
                    if k == 2:
                        for n in range(2):
                            pool.wait_ge(act_split, 4 * b + n + 1)
                            g.tensor_tensor(ropeb[:, n, :], ropea[:, n, :], parth[:, n, :], ALU.subtract).then_inc(pool_split, 1)
                    if k == 3:
                        for n in range(2):
                            pool.wait_ge(act_split, 4 * b + n + 3)
                            g.tensor_tensor(partl[:, n, :], ropeb[:, n, :], partm[:, n, :], ALU.subtract).then_inc(pool_split, 1)
                b = it - 2
                if 0 <= b < B:
                    if k == 1:
                        if b >= 2:
                            pool.wait_ge(sent[b % 2], 256 * (b // 2))
                        g.iota(xs[:, b % 2, :, :, C:C + 1].bitcast(I32).rearrange("p t s o -> p t (s o)"),
                               pattern=[[TOPK * P, TT], [1, TOPK]], base=TOPK * T * b,
                               channel_multiplier=TOPK).then_inc(meta_done, 1)
                    if k == 5:
                        pool.wait_ge(misc_free, job["RK", b] + 1)
                        if b:
                            pool.wait_ge(dest_seq, 2 * b)
                        g.tensor_tensor(prod[:, :, :, :], oh[:, :, :, :],
                                        rpos[:, :, :].unsqueeze(2).broadcast_to([P, TT, TOPK, NE]), ALU.mult).then_inc(prod_done, 1)
                b, c = scatter_chunk(it, k)
                if 0 <= b < B:
                    if c == 0:
                        pool.wait_ge(dest_seq, 2 * b + 2)
                        pool.wait_ge(xs_filled, TT * b + TT)
                        pool.wait_ge(meta_done, b + 1)
                    for n in (2 * c, 2 * c + 1):
                        g.indirect_dma_start(sorted_d[0][:, :], bass.IndirectOffsetOnAxis(dest[:, 16 * b + n:16 * b + n + 1], 0),
                                             xs[:, b % 2, n // TOPK, n % TOPK, :], None).then_inc(sent[b % 2], 16)


            pool.wait_ge(s2_ready, 5 * B * NP)
            pool.wait_ge(s1_ready, 5 * B * NP)
            g.memset(pads, 0.0).then_inc(pads_made, 1)
            pool.wait_ge(pads_made, 1)
            g.iota(pads.bitcast(I32).rearrange("p (r n) -> p r n", n=ROW)[:, :, C], pattern=[[0, 4]], base=NOWHERE,
                   channel_multiplier=0).then_inc(pads_made, 1)

            last_result = pool.to_reg(ROWS - 1)

            def experts(layer):
                base = GROUPS * layer

                def send(s, u, rnd):
                    pool.wait_ge(y_done, s + (base + 1))
                    g.nop(nofuse=True)
                    for i in range(G * u, G * u + G):
                        g.indirect_dma_start(result_d[layer][:, :], bass.IndirectOffsetOnAxis(xin[:, i, C:C + 1].bitcast(I32), 0),
                                             yout[:, i, :], None, bounds_check=last_result, oob_is_err=False).then_inc(y_sent[u], 16)

                expert_rounds(pool, send, 0)

            def scatters(b, first, end):
                for n in range(first, end):
                    g.indirect_dma_start(sorted_d[1][:, :], bass.IndirectOffsetOnAxis(dest[:, 16 * b + n:16 * b + n + 1], 0),
                                         xs[:, b % 2, n // TOPK, n % TOPK, :], None).then_inc(sent[b % 2], 16)

            g.memset(band, 1.0).then_inc(band_made, 1)
            pool.wait_ge(band_made, 1)
            g.affine_select(out=band, in_=band, compare_op=ALU.is_ge, fill=0.0, base=32,
                            pattern=[[-P, TT], [1, T]], channel_multiplier=-1).then_inc(band_made, 1)
            pool.wait_ge(band_made, 2)
            g.affine_select(out=band, in_=band, compare_op=ALU.is_ge, fill=0.0, base=31,
                            pattern=[[P, TT], [-1, T]], channel_multiplier=1).then_inc(band_made, 1)
            experts(0)
            for u in range(U):
                pool.wait_ge(y_sent[u], 16 * G * ROUNDS)
            g.memset(xs[:, :, :, :, C + 1:ROW], 0.0).then_inc(pads_made, 1)
            for b in range(-1, LAST_IT_B + 1):
                r, nxt = b - 1, b + 1
                if 0 <= r < B:
                    pool.wait_ge(ln3, 13 * r + 9)
                    g.tensor_tensor(rs1[:, :], rs1[:, :], mhalf[:, :], ALU.pow).then_inc(rstd3, 1)
                    pool.wait_ge(sent[r % 2], 256 * ((B + r) // 2))
                    g.iota(xs[:, r % 2, :, :, C:C + 1].bitcast(I32).rearrange("p t s o -> p t (s o)"),
                           pattern=[[TOPK * P, TT], [1, TOPK]], base=TOPK * T * r,
                           channel_multiplier=TOPK).then_inc(meta_done, 1)
                if 0 <= r - 1 < B:
                    pool.wait_ge(dest_seq, 2 * (B + r - 1) + 2)
                    pool.wait_ge(xs_filled, TT * (B + r - 1) + TT)
                    pool.wait_ge(meta_done, B + r)
                    pool.wait_ge(pads_made, 3)
                    scatters(r - 1, 0, 4)
                if nxt < B:
                    pool.wait_ge(ln2, 13 * nxt + 9)
                    g.tensor_tensor(rs0[:, :], rs0[:, :], mhalf[:, :], ALU.pow).then_inc(rstd2, 1)
                if 0 <= r - 1 < B:
                    scatters(r - 1, 4, 16)
                if 0 <= r < B:
                    bank, n = bjob["RK", r]
                    pool.wait_ge(bank_free[bank], n + 1)
                    pool.wait_ge(dest_seq, 2 * (B + r))
                    g.tensor_tensor(prod[:, :, :, :], oh[:, :, :, :],
                                    rpos[:, :, :].unsqueeze(2).broadcast_to([P, TT, TOPK, NE]), ALU.mult).then_inc(prod_done, 1)
            experts(1)


def kernel(**inputs):
    import numpy as np
    import concourse.bacc as bacc
    from concourse.bass_utils import run_bass_kernel_spmd

    a = {k: np.ascontiguousarray(v) for k, v in inputs.items()}
    swap = np.arange(C) ^ 1
    wa, ba = a["L0_attn_a_W_attn"], a["L0_attn_a_b_attn"]
    theta = (1.0 / np.float32(10000.0) ** (np.arange(0, HD, 2, dtype=np.float32) / np.float32(HD))).astype(np.float32)
    angle = (np.arange(C) // HD).astype(np.float32) * theta[(np.arange(C) % HD) // 2]
    sign = np.where(np.arange(C) % 2 == 0, -1.0, 1.0).astype(np.float32)
    trig = np.stack([np.cos(angle), np.sin(angle) * sign]).astype(np.float32)
    arrays = {
        "x": a["L0_attn_a_x"].reshape(B * T, C),
        "w": np.concatenate([wa[:, 0:C], wa[:, 0:C][:, swap], wa[:, C:2 * C], wa[:, C:2 * C][:, swap], wa[:, 2 * C:]], axis=1),
        "bcol": np.stack([ba[0:C], ba[0:C][swap], ba[C:2 * C], ba[C:2 * C][swap]], axis=1),
        "bv": ba[2 * C:],
        "wproj": a["L0_attn_a_W_proj"],
        "bproj": a["L0_attn_a_b_proj"],
        "trig_row": trig.reshape(2 * C),
        "trig_col": trig.T,
        "wb": np.concatenate([a["L0_attn_b_WQ"], a["L0_attn_b_WK"], a["L0_attn_b_WV"]], axis=1),
        "esel": a["L0_ffn_expert_sel"].T,
        "keys": a["L0_ffn_keys"],
        "values": a["L0_ffn_values"],
    }
    arrays = {f"in_{k}": np.ascontiguousarray(v) for k, v in arrays.items()}
    nc = bacc.Bacc("TRN2", target_bir_lowering=False, num_devices=1)
    args = [nc.dram_tensor(k, v.shape, F32, kind="ExternalInput").ap() for k, v in arrays.items()]
    out = nc.dram_tensor("out", (B * T, C), F32, kind="ExternalOutput").ap()
    build(nc, *args, out)
    r = run_bass_kernel_spmd(nc, [arrays], core_ids=[0])
    return r.results[0]["out"].reshape(B, T, C)
```
